# Optimizing a Trainium2 kernel written in Bass

```python
import numpy as np
import jax
import jax.numpy as jnp

def _softmax(x, axis=-1):
    return jax.nn.softmax(x, axis=axis)

def _gelu(x):
    return jax.nn.gelu(x, approximate=True)

def _silu(x):
    return jax.nn.silu(x)

def _sigmoid(x):
    return jax.nn.sigmoid(x)

def _layernorm(x, axis=-1, eps=1e-05):
    m = jnp.mean(x, axis=axis, keepdims=True)
    v = jnp.var(x, axis=axis, keepdims=True)
    return (x - m) / jnp.sqrt(v + eps)

def _scatter_add(tgt, idx, src, axis=0):
    return tgt.at[idx].add(src)

def _segment_sum(src, seg, n):
    return jax.ops.segment_sum(src, seg, n)
kernel_name = 'mk_gnn_preln_d4_gnn_r32_79894f'

def setup_inputs(seed: int=0):
    np.random.seed(seed)
    _w = jnp.asarray

    def _rec_inputs():
        import jax
        import jax.numpy as jnp
        _gk = jax.random.key(seed)
        x = -8.776e-05 + 1 * jax.random.normal(jax.random.fold_in(_gk, 1), (3125, 128), jnp.float32)
        src = jax.random.randint(jax.random.fold_in(_gk, 2), (100000,), 0, 3125, jnp.int32)
        dst = jax.random.randint(jax.random.fold_in(_gk, 3), (100000,), 0, 3125, jnp.int32)
        _o = jnp.argsort(dst, stable=True)
        src = src[_o]
        dst = dst[_o]
        return (x, src, dst)
    x, src, dst = _rec_inputs()

    def _L0_gnn_setup():
        import jax, jax.numpy as jnp
        import numpy as np
        EPS = 0.0
        N_NODES = 1250
        N_EDGES = 20000
        D_IN, D_HID, D_OUT = (128, 256, 128)
        key = jax.random.key(seed)
        k_x, k_e, k_w1, k_w2 = jax.random.split(key, 4)
        x = jax.random.normal(k_x, (N_NODES, D_IN), dtype=jnp.float32)
        edge_index = jax.random.randint(k_e, (2, N_EDGES), 0, N_NODES, dtype=jnp.int64)
        s1 = 1.0 / np.sqrt(D_IN)
        s2 = 1.0 / np.sqrt(D_HID)
        W1 = jax.random.normal(k_w1, (D_IN, D_HID), dtype=jnp.float32) * s1
        b1 = jnp.zeros((D_HID,), dtype=jnp.float32)
        W2 = jax.random.normal(k_w2, (D_HID, D_OUT), dtype=jnp.float32) * s2
        b2 = jnp.zeros((D_OUT,), dtype=jnp.float32)
        return {'x': x, 'edge_index': edge_index, 'W1': W1, 'b1': b1, 'W2': W2, 'b2': b2}
    _L0_gnn_all = _L0_gnn_setup()
    _L0_gnn_in = {k: v for k, v in _L0_gnn_all.items() if k in ('W1', 'b1', 'W2', 'b2')}
    del _L0_gnn_all

    def _L1_gnn_setup():
        import jax, jax.numpy as jnp
        import numpy as np
        N_NODES = 3125
        N_FEAT = 128
        HIDDEN = 16
        N_EDGES = 50000

        def gcn_conv(x, W, b, src, dst, n_nodes):
            ones = jnp.ones(src.shape[0], dtype=x.dtype)
            deg = jax.ops.segment_sum(ones, dst, num_segments=n_nodes)
            dinv = jnp.where(deg > 0, jax.lax.rsqrt(deg), 0.0)
            norm = dinv[src] * dinv[dst]
            h = x @ W
            msg = h[src] * norm[:, None]
            out = jax.ops.segment_sum(msg, dst, num_segments=n_nodes)
            return out + b
        key = jax.random.key(seed)
        k1, k2, k3, k4, k5, k6 = jax.random.split(key, 6)
        x = jax.random.normal(k1, (N_NODES, N_FEAT), dtype=jnp.float32)
        edge_index = jax.random.randint(k2, (2, N_EDGES), 0, N_NODES, dtype=jnp.int64)
        W1 = jax.random.normal(k3, (N_FEAT, HIDDEN), dtype=jnp.float32) / np.sqrt(N_FEAT)
        b1 = jnp.zeros((HIDDEN,), dtype=jnp.float32)
        W2 = jax.random.normal(k4, (HIDDEN, N_FEAT), dtype=jnp.float32) / np.sqrt(HIDDEN)
        b2 = jnp.zeros((N_FEAT,), dtype=jnp.float32)
        return {'x': x, 'edge_index': edge_index, 'W1': W1, 'b1': b1, 'W2': W2, 'b2': b2}
    _L1_gnn_all = _L1_gnn_setup()
    _L1_gnn_in = {k: v for k, v in _L1_gnn_all.items() if k in ('W1', 'b1', 'W2', 'b2')}
    del _L1_gnn_all

    def _L2_gnn_setup():
        import jax, jax.numpy as jnp
        import numpy as np
        N_NODES = 50000
        N_EDGES = 25000
        IN_CH = 128
        HEADS = 4
        OUT_CH = 32
        NEG_SLOPE = 0.2
        BN_EPS = 1e-05
        key = jax.random.key(seed)
        ks = jax.random.split(key, 8)
        x = jax.random.normal(ks[0], (N_NODES, IN_CH), dtype=jnp.float32)
        edge_index = jax.random.randint(ks[1], (2, N_EDGES), 0, N_NODES, dtype=jnp.int64 if jax.config.jax_enable_x64 else jnp.int32)
        W = jax.random.normal(ks[2], (IN_CH, HEADS * OUT_CH), dtype=jnp.float32) / np.sqrt(IN_CH)
        att_src = jax.random.normal(ks[3], (HEADS, OUT_CH), dtype=jnp.float32) * 0.1
        att_dst = jax.random.normal(ks[4], (HEADS, OUT_CH), dtype=jnp.float32) * 0.1
        bias = jnp.zeros((HEADS * OUT_CH,), dtype=jnp.float32)
        W_res = jax.random.normal(ks[5], (IN_CH, HEADS * OUT_CH), dtype=jnp.float32) / np.sqrt(IN_CH)
        bn_gamma = jnp.ones((HEADS * OUT_CH,), dtype=jnp.float32)
        bn_beta = jnp.zeros((HEADS * OUT_CH,), dtype=jnp.float32)
        bn_mean = jax.random.normal(ks[6], (HEADS * OUT_CH,), dtype=jnp.float32) * 0.1
        bn_var = jax.random.uniform(ks[7], (HEADS * OUT_CH,), dtype=jnp.float32, minval=0.5, maxval=1.5)
        return {'x': x, 'edge_index': edge_index, 'W': W, 'att_src': att_src, 'att_dst': att_dst, 'bias': bias, 'W_res': W_res, 'bn_gamma': bn_gamma, 'bn_beta': bn_beta, 'bn_mean': bn_mean, 'bn_var': bn_var}
    _L2_gnn_all = _L2_gnn_setup()
    _L2_gnn_in = {k: v for k, v in _L2_gnn_all.items() if k in ('W', 'att_src', 'att_dst', 'bias', 'W_res', 'bn_gamma', 'bn_beta', 'bn_mean', 'bn_var')}
    del _L2_gnn_all

    def _L3_gnn_setup():
        import jax, jax.numpy as jnp
        import numpy as np
        N_NODES = 3125
        N_EDGES = 50000
        NODE_DIM = 128
        HIDDEN = 128
        N_LAYERS = 4
        LN_EPS = 1e-05

        def _layernorm(x, g, b):
            mu = jnp.mean(x, axis=-1, keepdims=True)
            var = jnp.mean(jnp.square(x - mu), axis=-1, keepdims=True)
            return (x - mu) * jax.lax.rsqrt(var + LN_EPS) * g + b
        key = jax.random.key(seed)
        ks = jax.random.split(key, 16)
        s = 1.0 / np.sqrt(HIDDEN)
        inp = {'x': jax.random.normal(ks[0], (N_NODES, NODE_DIM), dtype=jnp.float32), 'edge_index': jax.random.randint(ks[1], (2, N_EDGES), 0, N_NODES, dtype=jnp.int64), 'Wn': jax.random.normal(ks[2], (NODE_DIM, HIDDEN), dtype=jnp.float32) / np.sqrt(NODE_DIM), 'bn': jnp.zeros((HIDDEN,), dtype=jnp.float32), 'WQ': jax.random.normal(ks[3], (N_LAYERS, HIDDEN, HIDDEN), dtype=jnp.float32) * s, 'bQ': jnp.zeros((N_LAYERS, HIDDEN), dtype=jnp.float32), 'WK': jax.random.normal(ks[4], (N_LAYERS, HIDDEN, HIDDEN), dtype=jnp.float32) * s, 'bK': jnp.zeros((N_LAYERS, HIDDEN), dtype=jnp.float32), 'WV': jax.random.normal(ks[5], (N_LAYERS, HIDDEN, HIDDEN), dtype=jnp.float32) * s, 'bV': jnp.zeros((N_LAYERS, HIDDEN), dtype=jnp.float32), 'WO': jax.random.normal(ks[6], (N_LAYERS, HIDDEN, HIDDEN), dtype=jnp.float32) * s, 'bO': jnp.zeros((N_LAYERS, HIDDEN), dtype=jnp.float32), 'ln_g': jnp.ones((N_LAYERS, HIDDEN), dtype=jnp.float32), 'ln_b': jnp.zeros((N_LAYERS, HIDDEN), dtype=jnp.float32), 'Wout': jax.random.normal(ks[7], (HIDDEN, NODE_DIM), dtype=jnp.float32) * s, 'bout': jnp.zeros((NODE_DIM,), dtype=jnp.float32)}
        return inp
    _L3_gnn_all = _L3_gnn_setup()
    _L3_gnn_in = {k: v for k, v in _L3_gnn_all.items() if k in ('Wn', 'bn', 'WQ', 'bQ', 'WK', 'bK', 'WV', 'bV', 'WO', 'bO', 'ln_g', 'ln_b', 'Wout', 'bout')}
    del _L3_gnn_all
    return {'x': x, 'src': src, 'dst': dst, 'L0_gnn_W1': _L0_gnn_in['W1'], 'L0_gnn_b1': _L0_gnn_in['b1'], 'L0_gnn_W2': _L0_gnn_in['W2'], 'L0_gnn_b2': _L0_gnn_in['b2'], 'L1_gnn_W1': _L1_gnn_in['W1'], 'L1_gnn_b1': _L1_gnn_in['b1'], 'L1_gnn_W2': _L1_gnn_in['W2'], 'L1_gnn_b2': _L1_gnn_in['b2'], 'L2_gnn_W': _L2_gnn_in['W'], 'L2_gnn_att_src': _L2_gnn_in['att_src'], 'L2_gnn_att_dst': _L2_gnn_in['att_dst'], 'L2_gnn_bias': _L2_gnn_in['bias'], 'L2_gnn_W_res': _L2_gnn_in['W_res'], 'L2_gnn_bn_gamma': _L2_gnn_in['bn_gamma'], 'L2_gnn_bn_beta': _L2_gnn_in['bn_beta'], 'L2_gnn_bn_mean': _L2_gnn_in['bn_mean'], 'L2_gnn_bn_var': _L2_gnn_in['bn_var'], 'L3_gnn_Wn': _L3_gnn_in['Wn'], 'L3_gnn_bn': _L3_gnn_in['bn'], 'L3_gnn_WQ': _L3_gnn_in['WQ'], 'L3_gnn_bQ': _L3_gnn_in['bQ'], 'L3_gnn_WK': _L3_gnn_in['WK'], 'L3_gnn_bK': _L3_gnn_in['bK'], 'L3_gnn_WV': _L3_gnn_in['WV'], 'L3_gnn_bV': _L3_gnn_in['bV'], 'L3_gnn_WO': _L3_gnn_in['WO'], 'L3_gnn_bO': _L3_gnn_in['bO'], 'L3_gnn_ln_g': _L3_gnn_in['ln_g'], 'L3_gnn_ln_b': _L3_gnn_in['ln_b'], 'L3_gnn_Wout': _L3_gnn_in['Wout'], 'L3_gnn_bout': _L3_gnn_in['bout']}

def reference(x, src, dst, L0_gnn_W1, L0_gnn_b1, L0_gnn_W2, L0_gnn_b2, L1_gnn_W1, L1_gnn_b1, L1_gnn_W2, L1_gnn_b2, L2_gnn_W, L2_gnn_att_src, L2_gnn_att_dst, L2_gnn_bias, L2_gnn_W_res, L2_gnn_bn_gamma, L2_gnn_bn_beta, L2_gnn_bn_mean, L2_gnn_bn_var, L3_gnn_Wn, L3_gnn_bn, L3_gnn_WQ, L3_gnn_bQ, L3_gnn_WK, L3_gnn_bK, L3_gnn_WV, L3_gnn_bV, L3_gnn_WO, L3_gnn_bO, L3_gnn_ln_g, L3_gnn_ln_b, L3_gnn_Wout, L3_gnn_bout):
    import jax
    import jax.numpy as jnp

    def _L0_gnn_ref(x, edge_index, W1, b1, W2, b2):
        import jax, jax.numpy as jnp
        import numpy as np
        EPS = 0.0
        N_NODES = 1250
        N_EDGES = 20000
        D_IN, D_HID, D_OUT = (128, 256, 128)
        row, col = (edge_index[0], edge_index[1])
        keep = (row != col).astype(x.dtype)[:, None]
        gathered = x[col] * keep
        agg = jax.ops.segment_sum(gathered, row, num_segments=x.shape[0])
        out = (1.0 + EPS) * x + agg
        h = jax.nn.relu(out @ W1 + b1)
        return h @ W2 + b2

    def _L1_gnn_ref(x, edge_index, W1, b1, W2, b2):
        import jax, jax.numpy as jnp
        import numpy as np
        N_NODES = 3125
        N_FEAT = 128
        HIDDEN = 16
        N_EDGES = 50000

        def gcn_conv(x, W, b, src, dst, n_nodes):
            ones = jnp.ones(src.shape[0], dtype=x.dtype)
            deg = jax.ops.segment_sum(ones, dst, num_segments=n_nodes)
            dinv = jnp.where(deg > 0, jax.lax.rsqrt(deg), 0.0)
            norm = dinv[src] * dinv[dst]
            h = x @ W
            msg = h[src] * norm[:, None]
            out = jax.ops.segment_sum(msg, dst, num_segments=n_nodes)
            return out + b
        n = x.shape[0]
        loops = jnp.arange(n, dtype=edge_index.dtype)
        src = jnp.concatenate([edge_index[0], loops])
        dst = jnp.concatenate([edge_index[1], loops])
        h = gcn_conv(x, W1, b1, src, dst, n)
        h = jax.nn.relu(h)
        h = gcn_conv(h, W2, b2, src, dst, n)
        return jax.nn.log_softmax(h, axis=1)

    def _L2_gnn_ref(x, edge_index, W, att_src, att_dst, bias, W_res, bn_gamma, bn_beta, bn_mean, bn_var):
        import jax, jax.numpy as jnp
        import numpy as np
        N_NODES = 50000
        N_EDGES = 25000
        IN_CH = 128
        HEADS = 4
        OUT_CH = 32
        NEG_SLOPE = 0.2
        BN_EPS = 1e-05
        N = x.shape[0]
        H, C = att_src.shape
        loops = jnp.arange(N, dtype=edge_index.dtype)
        src = jnp.concatenate([edge_index[0], loops])
        dst = jnp.concatenate([edge_index[1], loops])
        h = (x @ W).reshape(N, H, C)
        a_src = jnp.einsum('nhc,hc->nh', h, att_src)
        a_dst = jnp.einsum('nhc,hc->nh', h, att_dst)
        logits = jax.nn.leaky_relu(a_src[src] + a_dst[dst], NEG_SLOPE)
        m = jax.lax.stop_gradient(jax.ops.segment_max(logits, dst, num_segments=N))
        e = jnp.exp(logits - m[dst])
        s = jax.ops.segment_sum(e, dst, num_segments=N)
        alpha = e / s[dst]
        msg = h[src] * alpha[:, :, None]
        out = jax.ops.segment_sum(msg, dst, num_segments=N).reshape(N, H * C)
        out = out + x @ W_res + bias
        out = (out - bn_mean) * jax.lax.rsqrt(bn_var + BN_EPS) * bn_gamma + bn_beta
        return jax.nn.elu(out)

    def _L3_gnn_ref(x, edge_index, Wn, bn, WQ, bQ, WK, bK, WV, bV, WO, bO, ln_g, ln_b, Wout, bout):
        import jax, jax.numpy as jnp
        import numpy as np
        N_NODES = 3125
        N_EDGES = 50000
        NODE_DIM = 128
        HIDDEN = 128
        N_LAYERS = 4
        LN_EPS = 1e-05

        def _layernorm(x, g, b):
            mu = jnp.mean(x, axis=-1, keepdims=True)
            var = jnp.mean(jnp.square(x - mu), axis=-1, keepdims=True)
            return (x - mu) * jax.lax.rsqrt(var + LN_EPS) * g + b
        n = x.shape[0]
        src, dst = (edge_index[0], edge_index[1])
        scale = 1.0 / np.sqrt(HIDDEN)
        h = x @ Wn + bn
        for l in range(N_LAYERS):
            Q = h @ WQ[l] + bQ[l]
            K = h @ WK[l] + bK[l]
            V = h @ WV[l] + bV[l]
            scores = jnp.sum(Q[dst] * K[src], axis=-1) * scale
            seg_max = jax.ops.segment_max(scores, dst, num_segments=n)
            e = jnp.exp(scores - seg_max[dst])
            seg_sum = jax.ops.segment_sum(e, dst, num_segments=n)
            attn = e / seg_sum[dst]
            messages = jax.ops.segment_sum(attn[:, None] * V[src], dst, num_segments=n)
            out = messages @ WO[l] + bO[l]
            h = _layernorm(h + out, ln_g[l], ln_b[l])
        return h @ Wout + bout
    edge_index = jnp.stack([src, dst])
    h = jnp.maximum(_layernorm(x, axis=-1), 0.0)
    x = x + _L0_gnn_ref(h, edge_index, L0_gnn_W1, L0_gnn_b1, L0_gnn_W2, L0_gnn_b2)
    h = jnp.maximum(_layernorm(x, axis=-1), 0.0)
    x = x + _L1_gnn_ref(h, edge_index, L1_gnn_W1, L1_gnn_b1, L1_gnn_W2, L1_gnn_b2)
    h = jnp.maximum(_layernorm(x, axis=-1), 0.0)
    x = x + _L2_gnn_ref(h, edge_index, L2_gnn_W, L2_gnn_att_src, L2_gnn_att_dst, L2_gnn_bias, L2_gnn_W_res, L2_gnn_bn_gamma, L2_gnn_bn_beta, L2_gnn_bn_mean, L2_gnn_bn_var)
    h = jnp.maximum(_layernorm(x, axis=-1), 0.0)
    x = x + _L3_gnn_ref(h, edge_index, L3_gnn_Wn, L3_gnn_bn, L3_gnn_WQ, L3_gnn_bQ, L3_gnn_WK, L3_gnn_bK, L3_gnn_WV, L3_gnn_bV, L3_gnn_WO, L3_gnn_bO, L3_gnn_ln_g, L3_gnn_ln_b, L3_gnn_Wout, L3_gnn_bout)
    return x

_drawn_inputs = setup_inputs


def setup_inputs(seed=0):
    import zlib

    import numpy as np

    out = dict(_drawn_inputs(seed))
    spreads = {'L0_gnn_b1': (0.0, 0.8),
     'L0_gnn_b2': (0.0, 0.8),
     'L1_gnn_b1': (0.0, 0.794),
     'L1_gnn_b2': (0.0, 0.73),
     'L2_gnn_bias': (0.0, 0.8),
     'L2_gnn_bn_gamma': (1.0, 0.6),
     'L2_gnn_bn_beta': (0.0, 0.8),
     'L3_gnn_bn': (0.0, 0.8),
     'L3_gnn_bQ': (0.0, 0.8),
     'L3_gnn_bK': (0.0, 0.8),
     'L3_gnn_bV': (0.0, 0.548),
     'L3_gnn_bO': (0.0, 0.621),
     'L3_gnn_ln_g': (1.0, 0.2),
     'L3_gnn_ln_b': (0.0, 0.455),
     'L3_gnn_bout': (0.0, 0.8)}
    factors = {'L2_gnn_att_src': 8.0,
     'L2_gnn_att_dst': 8.0,
     'L2_gnn_bn_mean': 6.121,
     'L2_gnn_bn_var': 5.496,
     'L3_gnn_WQ': 8.0,
     'L3_gnn_WK': 8.0}
    for name, (base, spread) in spreads.items():
        noise = np.random.default_rng([zlib.crc32(name.encode()), seed]).standard_normal(out[name].shape)
        drawn = base * np.exp(spread * noise) if base else spread * noise
        out[name] = jnp.asarray(drawn.astype(out[name].dtype))
    for name, factor in factors.items():
        out[name] = (out[name] * factor).astype(out[name].dtype)
    return out
```

```python
from contextlib import ExitStack

import numpy as np

import concourse.bass as bass
from concourse import mybir

FP32, BF16, FP16, I32 = mybir.dt.float32, mybir.dt.bfloat16, mybir.dt.float16, mybir.dt.int32
ALU = mybir.AluOpType
ACT = mybir.ActivationFunctionType
AX = mybir.AxisListType

N, E, D = 3125, 100000, 128
T = 125
NT = N // T
C4 = 4 * T
CHUNKS = [(c * C4, min(N, (c + 1) * C4)) for c in range((N + C4 - 1) // C4)]
NC = len(CHUNKS)
NO_EDGE = -1.0e30
EP = 128
PAIR = 4 * EP
NPAIR = (E + PAIR - 1) // PAIR
ROWS = NPAIR // 2
W = 12
WN = W * NT
SLOTS = W + T + W
LAST = E - (ROWS - 1) * 2 * PAIR
LASTG = E - (E // (PAIR // 2)) * (PAIR // 2)
ROUND = 12582912.0
S_PAD = 100000000


class Marks:
    def __init__(self, sem):
        self.sem, self.n = sem, 0

    def inc(self, ins, by=1):
        ins.then_inc(self.sem, by)
        self.n += by
        return self.n


def chain(eng, marks, ins):
    eng.wait_ge(marks.sem, marks.inc(ins))


def pairs_of_blocks(eng, step):
    with eng.Fori(0, NT // 2) as i:
        step(2 * i, 0, i)
        step(2 * i + 1, 1, i)
    step(NT - 1, 0, NT // 2)


def roots(act, stat, var_ready, root_ready):
    act.wait_ge(var_ready, 1)
    act.activation(stat[:, 1, :], stat[:, 1, :], ACT.Sqrt).then_inc(root_ready, 1)


def layer_norm(dve, m, x, h, work, stat, var_ready, root_ready):
    mean, var = stat[:, 0, :], stat[:, 1, :]
    chain(dve, m, dve.tensor_reduce(mean, x, AX.X, ALU.add))
    chain(dve, m, dve.tensor_scalar(mean, mean, 1.0 / D, None, ALU.mult))
    chain(dve, m, dve.tensor_tensor(h, x, mean.unsqueeze(2).broadcast_to([T, NT, D]), ALU.subtract))
    chain(dve, m, dve.tensor_tensor(work, h, h, ALU.mult))
    chain(dve, m, dve.tensor_reduce(var, work, AX.X, ALU.add))
    dve.tensor_scalar(var, var, 1.0 / D, 1e-5, ALU.mult, ALU.add).then_inc(var_ready, 1)
    dve.wait_ge(root_ready, 1)
    chain(dve, m, dve.reciprocal(var, var))
    chain(dve, m, dve.tensor_tensor(h, h, var.unsqueeze(2).broadcast_to([T, NT, D]), ALU.mult))


def layer_norm_relu(dve, m, x, h, work, stat, var_ready, root_ready):
    layer_norm(dve, m, x, h, work, stat, var_ready, root_ready)
    chain(dve, m, dve.tensor_scalar(h, h, 0.0, None, ALU.max))


def prepare(nc, G):
    with ExitStack() as ctx:
        sb = lambda name, shape, dt=FP32: ctx.enter_context(nc.sbuf_tensor(name, shape, dt))
        ps = lambda name, shape, dt=FP32: ctx.enter_context(nc.psum_tensor(name, shape, dt))
        sem = lambda name: ctx.enter_context(nc.semaphore(name))
        d_i = sb("d_i", [ROWS, 2 * PAIR], I32)
        s_i = sb("s_i", [ROWS, 2 * PAIR], I32)
        d_f = sb("d_f", [ROWS, 2 * PAIR])
        s_f = sb("s_f", [ROWS, 2 * PAIR])
        tile_f = sb("tile_f", [ROWS, 2 * PAIR])
        gmm = sb("gmm", [ROWS, 2, 4])
        rows = sb("rows", [NT, 2, 2 * NPAIR])
        pmin = sb("pmin", [NT, NPAIR])
        pmax = sb("pmax", [NT, NPAIR])
        pidx = sb("pidx", [NT, NPAIR])
        bidx = sb("bidx", [NT, 1])
        bnd = sb("bnd", [NT, 2])
        tab = sb("tab", [NT, 3])
        tab_i = sb("tab_i", [NT, 3], I32)
        spn = sb("spn", [NT, 2 * NPAIR])
        work = sb("ln_work", [T, NT, D])
        stat = sb("ln_stat", [T, 2, NT])
        key_ps = ps("key_ps", [EP, 2, 512])
        sp_ps = ps("sp_ps", [EP, 2, 512])
        edges_in = sem("edges_in")
        x_in = sem("x_in")
        s_padded = sem("s_padded")
        consts_ready = sem("consts_ready")
        dve_done = sem("prep_dve_done")
        mm_out = sem("mm_out")
        mm_back = sem("mm_back")
        tab_out = sem("tab_out")
        tab_back = sem("tab_back")
        keys_ready = sem("keys_ready")
        mm_ready = sem("mm_ready")
        tab_ready = sem("tab_ready")
        turned = sem("turned")
        var_ready = sem("var_ready0")
        root_ready = sem("root_ready0")
        x, h, ident = G["x"], G["h"], G["ident"]
        with nc.Block() as block:
            @block.sync
            def _(sp):
                full = (ROWS - 1) * 2 * PAIR
                def rows_of(a, lo, n):
                    return a[lo:lo + n].rearrange("(a n) -> a n", a=1)
                sp.dma_start(d_i[0:ROWS - 1, :], G["dst"][0:full].rearrange("(p n) -> p n", n=2 * PAIR)).then_inc(edges_in, 16)
                sp.dma_start(d_i[ROWS - 1:ROWS, 0:LAST], rows_of(G["dst"], full, LAST)).then_inc(edges_in, 16)
                at = LAST
                while at < 2 * PAIR:
                    n = min(LASTG, 2 * PAIR - at)
                    sp.dma_start(d_i[ROWS - 1:ROWS, at:at + n], rows_of(G["dst"], E - LASTG, n)).then_inc(edges_in, 16)
                    at += n
                sp.wait_ge(s_padded, 1)
                sp.dma_start(s_i[0:ROWS - 1, :], G["src"][0:full].rearrange("(p n) -> p n", n=2 * PAIR)).then_inc(edges_in, 16)
                sp.dma_start(s_i[ROWS - 1:ROWS, 0:LAST], rows_of(G["src"], full, LAST)).then_inc(edges_in, 16)
                sp.dma_start(x[:, :, :], G["x_in"].rearrange("(t p) d -> p t d", p=T)).then_inc(x_in, 16)
                sp.wait_ge(mm_ready, 1)
                sp.dma_start(G["mm_dram"].rearrange("k (p q) -> p k q", q=4), gmm[:, :, :]).then_inc(mm_out, 16)
                sp.wait_ge(mm_out, 16)
                sp.dma_start(rows[:, :, :], G["mm_dram"].unsqueeze(0).broadcast_to([NT, 2, 2 * NPAIR])).then_inc(mm_back, 16)
                sp.dma_start(G["gmin"][0:1, :], G["mm_dram"][0:1, :]).then_inc(mm_back, 16)
                sp.wait_ge(tab_ready, 1)
                sp.dma_start(G["tab_dram"][:, :], tab_i[:, :]).then_inc(tab_out, 16)
                sp.wait_ge(tab_out, 16)
                sp.dma_start(G["ranges"][0:1, :], G["tab_dram"].rearrange("(a b) c -> a (b c)", a=1)).then_inc(tab_back, 16)
                sp.wait_ge(tab_back, 16)

            @block.gpsimd
            def _(pool):
                pool.memset(s_i[:, PAIR:], S_PAD).then_inc(s_padded, 1)
                pool.memset(ident[:, :], 0.0).then_inc(consts_ready, 1)
                pool.wait_ge(consts_ready, 1)
                pool.affine_select(out=ident[:, :], in_=ident[:, :], compare_op=ALU.not_equal, fill=1.0,
                                   base=0, pattern=[[-1, 128]], channel_multiplier=1).then_inc(consts_ready, 1)
                pool.iota(G["iota_win"][:, :], [[1, WN]], base=0, channel_multiplier=0,
                          allow_small_or_imprecise_dtypes=True).then_inc(consts_ready, 1)
                pool.iota(G["iota_t"][:, :, :], [[0, 2], [1, T]], base=0, channel_multiplier=0,
                          allow_small_or_imprecise_dtypes=True).then_inc(consts_ready, 1)
                pool.iota(pidx[:, :], [[1, NPAIR]], base=0, channel_multiplier=0,
                          allow_small_or_imprecise_dtypes=True).then_inc(consts_ready, 1)
                pool.iota(bidx[:, :], [[0, 1]], base=0, channel_multiplier=T,
                          allow_small_or_imprecise_dtypes=True).then_inc(consts_ready, 1)
                pool.memset(G["tiny"][:, :], 2.0 ** -60).then_inc(consts_ready, 1)
                pool.memset(G["lift"][:, :], 2.0e29).then_inc(consts_ready, 1)
                pool.memset(G["agg"][:, :], 0.0).then_inc(consts_ready, 1)

            @block.scalar
            def _(act):
                roots(act, stat, var_ready, root_ready)

            @block.vector
            def _(dve):
                m = Marks(dve_done)
                dve.wait_ge(edges_in, 16 * 7)
                q4 = lambda t: t[:, :].rearrange("p (q n) -> p q n", q=4)
                chain(dve, m, dve.tensor_copy(d_f[:, :], d_i[:, :]))
                chain(dve, m, dve.tensor_reduce(gmm[:, 0, :], q4(d_f), AX.X, ALU.min))
                dve.tensor_reduce(gmm[:, 1, :], q4(d_f), AX.X, ALU.max).then_inc(mm_ready, 1)
                chain(dve, m, dve.tensor_copy(s_f[:, :], s_i[:, :]))
                chain(dve, m, dve.tensor_scalar(tile_f[:, :], s_f[:, :], 1.0 / T, 0.5 / T - 0.5, ALU.mult, ALU.add))
                chain(dve, m, dve.tensor_scalar(tile_f[:, :], tile_f[:, :], ROUND, None, ALU.add))
                chain(dve, m, dve.tensor_scalar(tile_f[:, :], tile_f[:, :], ROUND, None, ALU.subtract))
                chain(dve, m, dve.scalar_tensor_tensor(out=s_f[:, :], in0=tile_f[:, :], scalar=-float(T), in1=s_f[:, :],
                                                       op0=ALU.mult, op1=ALU.add))
                chain(dve, m, dve.tensor_tensor(q4(d_f), q4(d_f), gmm[:, 0, :].unsqueeze(2).broadcast_to([ROWS, 4, 2 * EP]),
                                                ALU.subtract))
                dve.scalar_tensor_tensor(out=d_f[:, :], in0=d_f[:, :], scalar=float(NT), in1=tile_f[:, :],
                                         op0=ALU.mult, op1=ALU.add).then_inc(keys_ready, 1)
                for j in range(2):
                    for k, (bank, out) in enumerate(((key_ps, G["key"]), (sp_ps, G["place"]))):
                        dve.wait_ge(turned, 2 * j + k + 1)
                        dve.tensor_copy(out[:, :].rearrange("e (p j i) -> e j i p", j=2, i=4)[:, j],
                                        bank[:, j, 0:4 * ROWS].rearrange("e (i p) -> e i p", i=4))
                dve.wait_ge(consts_ready, 9)
                dve.wait_ge(mm_back, 32)
                both = rows[:, :, :].rearrange("b k (p g) -> b k p g", g=2)
                chain(dve, m, dve.tensor_reduce(pmin[:, :], both[:, 0], AX.X, ALU.min))
                chain(dve, m, dve.tensor_reduce(pmax[:, :], both[:, 1], AX.X, ALU.max))
                chain(dve, m, dve.tensor_scalar(bnd[:, 0:1], bidx[:, :], float(T - 1), None, ALU.add))
                chain(dve, m, dve.tensor_scalar(pmax[:, :], pmax[:, :], bidx[:, 0:1], 1000.0, ALU.is_lt, ALU.mult))
                chain(dve, m, dve.tensor_tensor(pmax[:, :], pmax[:, :], pidx[:, :], ALU.add))
                chain(dve, m, dve.tensor_reduce(tab[:, 0:1], pmax[:, :], AX.X, ALU.min))
                chain(dve, m, dve.tensor_scalar(pmin[:, :], pmin[:, :], bnd[:, 0:1], None, ALU.is_le))
                chain(dve, m, dve.tensor_scalar(pidx[:, :], pidx[:, :], 1.0, None, ALU.add))
                chain(dve, m, dve.tensor_tensor(pmin[:, :], pmin[:, :], pidx[:, :], ALU.mult))
                chain(dve, m, dve.tensor_reduce(tab[:, 1:2], pmin[:, :], AX.X, ALU.max))
                chain(dve, m, dve.tensor_scalar(tab[:, 0:1], tab[:, 0:1], float(NPAIR - 1), None, ALU.min))
                chain(dve, m, dve.tensor_scalar(bnd[:, 1:2], tab[:, 0:1], 1.0, None, ALU.add))
                chain(dve, m, dve.tensor_tensor(tab[:, 1:2], tab[:, 1:2], bnd[:, 1:2], ALU.max))
                chain(dve, m, dve.tensor_tensor(spn[:, :], rows[:, 1, :], rows[:, 0, :], ALU.subtract))
                chain(dve, m, dve.tensor_reduce(tab[:, 2:3], spn[:, :], AX.X, ALU.max))
                chain(dve, m, dve.tensor_scalar(tab[:, 2:3], tab[:, 2:3], 1.0 / W, 0.5 / W - 0.5, ALU.mult, ALU.add))
                chain(dve, m, dve.tensor_scalar(tab[:, 2:3], tab[:, 2:3], ROUND, None, ALU.add))
                chain(dve, m, dve.tensor_scalar(tab[:, 2:3], tab[:, 2:3], ROUND - 1.0, None, ALU.subtract))
                dve.tensor_copy(tab_i[:, :], tab[:, :]).then_inc(tab_ready, 1)
                dve.tensor_scalar(G["gmin"][0:1, :], G["gmin"][0:1, :], float(W), None, ALU.add)
                dve.wait_ge(x_in, 16)
                layer_norm_relu(dve, m, x[:, :, :], h[:, :, :], work[:, :, :], stat, var_ready, root_ready)

            @block.tensor
            def _(pe):
                pe.wait_ge(consts_ready, 2)
                pe.wait_ge(keys_ready, 1)
                for j in range(2):
                    for bank, src in ((key_ps, d_f), (sp_ps, s_f)):
                        for i in range(4):
                            at = j * PAIR + i * EP
                            last = pe.transpose(bank[:, j, i * ROWS:(i + 1) * ROWS], src[:, at:at + EP],
                                                ident[0:ROWS, 0:ROWS])
                        last.then_inc(turned, 1)


def build_counts(nc, G):
    with ExitStack() as ctx:
        sb = lambda name, shape, dt=FP32: ctx.enter_context(nc.sbuf_tensor(name, shape, dt))
        ps = lambda name, shape, dt=FP32: ctx.enter_context(nc.psum_tensor(name, shape, dt))
        sem = lambda name: ctx.enter_context(nc.semaphore(name))
        blk = [sb(f"blk{p}", [T, SLOTS * NT]) for p in range(2)]
        lnrow = [sb(f"lnrow{p}", [T, N]) for p in range(2)]
        liftrow = sb("liftrow", [T, N])
        hot_key = sb("hot_key", [EP, 4, WN], BF16)
        off_place = sb("off_place", [EP, 4, T], FP16)
        hot_place = sb("hot_place", [EP, 4, T], BF16)
        posf = sb("posf", [1, 2 * NPAIR])
        posi = sb("posi", [1, 2 * NPAIR], I32)
        shift = sb("shift", [EP, 1])
        dtile = sb("dtile", [T, T])
        win = [ps(f"win{k}", [T, WN]) for k in range(2)]
        turn = [ps(f"turn{k}", [T, C4]) for k in range(2)]
        acc = [ps(f"acc{k}", [D, C4]) for k in range(2)]
        crow = sb("crow", [T, N])
        deg_parts = [sb(f"deg_parts{p}", [T, NC]) for p in range(2)]
        h_tile = [sb(f"h_tile{p}", [T, D]) for p in range(2)]
        ranges, h, sums, ident = G["ranges"], G["h"], G["agg"], G["ident"]
        off_ready = sem("off_ready")
        off_read = sem("off_read")
        hot_key_ready = sem("hot_key_ready")
        group_done = sem("group_done")
        added = sem("added")
        pos_made = sem("pos_made")
        passed = G["passed"]
        blk_zero = sem("blk_zero")
        blk_full = sem("blk_full")
        blk_used = sem("blk_used")
        counts_out = [sem(f"counts_out{p}") for p in range(2)]
        turn_ready = sem("turn_ready")
        ln_in = sem("ln_in")
        min_done = sem("min_done")
        bank_read = sem("bank_read")
        part_filled = sem("part_filled")
        part_added = sem("part_added")
        h_staged = sem("h_staged")
        deg_done = sem("deg_done")
        ln_ready = sem("ln_ready")
        bias_out = [sem(f"bias_out{p}") for p in range(2)]
        diag_ready = sem("diag_ready")
        diag_read = sem("diag_read")

        def ranges_of(eng, b):
            lo = eng.value_load(ranges[0:1, bass.ds(3 * b, 1)], min_val=0, max_val=NPAIR - 1)
            hi = eng.value_load(ranges[0:1, bass.ds(3 * b + 1, 1)], min_val=1, max_val=NPAIR)
            return lo, hi

        def over_pairs(eng, b, turns, rounds, body):
            lo, hi = ranges_of(eng, b)
            with eng.Fori(0, rounds) as _:
                with eng.Fori(lo, hi) as pair:
                    it = eng.snap(turns, min_val=0, max_val=2 ** 24)
                    body(pair, it)
                    eng.reg_add(turns, turns, 1)

        def start(eng):
            turns = eng.alloc_register("turns")
            eng.reg_mov(turns, 0)
            rounds = eng.value_load(ranges[0:1, 2:3], min_val=1, max_val=(N + W - 1) // W + 1)
            return turns, rounds

        with nc.Block() as block:
            @block.sync
            def _(sp):
                for p in range(2):
                    sp.sem_inc(counts_out[p], 16)
                    sp.sem_inc(bias_out[p], 16)

                def step(b, p, i2):
                    sp.wait_ge(blk_full, b + 1)
                    sp.dma_start(G["counts_dram"][b, :, :], blk[p][:, WN:WN + N]).then_inc(counts_out[p], 16)
                    sp.wait_ge(min_done, b * NC + NC)
                    sp.dma_start(G["bias_dram"][b, :, :], lnrow[p][:, :]).then_inc(bias_out[p], 16)
                pairs_of_blocks(sp, step)
                for p in range(2):
                    blocks = (NT + 1 - p) // 2
                    sp.wait_ge(counts_out[p], 16 * (blocks + 1))
                    sp.wait_ge(bias_out[p], 16 * (blocks + 1))

            @block.gpsimd
            def _(pool):
                turns, rounds = start(pool)

                def step(b, p, i2):
                    pool.wait_ge(blk_used, b + 1)
                    pool.wait_ge(counts_out[p], 16 * i2 + 16)
                    pool.wait_ge(diag_read, b)
                    pool.sem_inc(passed, 1)
                    pool.memset(blk[p][:, :], 0.0).then_inc(blk_zero, 1)

                    def body(pair, it):
                        for k in range(2):
                            pool.wait_ge(off_read, 2 * it + (k + 1))
                            pool.tensor_tensor(
                                off_place[:, 2 * k:2 * k + 2, :], G["iota_t"][:, :, :],
                                G["place"][:, bass.ds(pair * 4 + 2 * k, 2)].unsqueeze(2).broadcast_to([EP, 2, T]),
                                ALU.subtract).then_inc(off_ready, 1)
                    over_pairs(pool, b, turns, rounds, body)
                    pool.wait_ge(part_filled, b * NC)
                    pool.tensor_copy(h_tile[p][:, :].unsqueeze(1), h[:, bass.ds(b, 1), :]).then_inc(h_staged, 1)
                    pool.wait_ge(blk_full, b + 1)
                    on = blk[p][:, WN:WN + N].rearrange("p (d t) -> p d t", t=NT)[:, :, bass.ds(b, 1)]
                    pool.tensor_tensor(dtile[:, :].unsqueeze(2), on, ident[0:T, 0:T].unsqueeze(2), ALU.mult).then_inc(diag_ready, 1)
                pairs_of_blocks(pool, step)

            @block.vector
            def _(dve):
                turns, rounds = start(dve)
                inner = dve.alloc_register("pos_turns")
                dve.reg_mov(inner, 0)
                dve.sem_inc(added, 2)
                dve.sem_inc(part_added, 2)
                dve.sem_inc(deg_done, 2)
                dve.sem_inc(off_read, 2)
                base = G["gmin"]

                def step(b, p, i2):
                    def made(k):
                        dve.wait_ge(pos_made, 3 * dve.snap(inner, min_val=0, max_val=2 ** 24) + (3 * b + k))
                    made(0)
                    dve.tensor_copy(posf[:, :], base[0:1, :]).then_inc(pos_made, 1)
                    dve.memset(shift[:, :], 0.0).then_inc(pos_made, 1)
                    lo, hi = ranges_of(dve, b)
                    dve.wait_ge(blk_zero, b + 1)
                    dve.sem_inc(passed, 1)
                    with dve.Fori(0, rounds) as _:
                        made(2)
                        dve.tensor_scalar(posi[:, :], posf[:, :], 0.0, float(W + T), ALU.max, ALU.min).then_inc(pos_made, 1)
                        made(3)
                        dve.sem_inc(passed, 1)
                        with dve.Fori(lo, hi) as pair:
                            it = dve.snap(turns, min_val=0, max_val=2 ** 24)
                            pos = [dve.value_load(posi[0:1, bass.ds(pair * 2 + k, 1)], min_val=0, max_val=W + T)
                                   for k in range(2)]
                            for k in range(2):
                                for i in (2 * k, 2 * k + 1):
                                    one = dve.tensor_scalar(hot_key[:, i, :], G["iota_win"][:, :],
                                                            G["key"][:, bass.ds(pair * 4 + i, 1)], shift[:, 0:1],
                                                            ALU.subtract, ALU.is_equal)
                                dve.wait_ge(off_ready, 2 * it + (k + 1))
                                dve.tensor_scalar(hot_place[:, 2 * k:2 * k + 2, :], off_place[:, 2 * k:2 * k + 2, :],
                                                  0.0, None, ALU.is_equal).then_inc(off_read, 1)
                                dve.wait_ge(off_read, 2 * it + (k + 3))
                                dve.sem_inc(hot_key_ready, 1)
                            for k in range(2):
                                dve.wait_ge(group_done, 2 * it + (k + 3))
                                dve.wait_ge(added, 2 * it + (k + 2))
                                here = blk[p][:, bass.ds(pos[k] * NT, WN)]
                                dve.tensor_tensor(here, here, win[k][:, :], ALU.add).then_inc(added, 1)
                            dve.reg_add(turns, turns, 1)
                        dve.tensor_scalar(posf[:, :], posf[:, :], float(W), None, ALU.add).then_inc(pos_made, 1)
                        dve.tensor_scalar(shift[:, :], shift[:, :], float(WN), None, ALU.subtract).then_inc(pos_made, 1)
                        dve.reg_add(inner, inner, 1)
                    it = dve.snap(turns, min_val=0, max_val=2 ** 24)
                    dve.wait_ge(added, 2 * it + 2)
                    dve.sem_inc(blk_full, 1)
                    dve.tensor_scalar(base[0:1, :], base[0:1, :], float(T), None, ALU.subtract).then_inc(pos_made, 1)
                    for c, (a, z) in enumerate(CHUNKS):
                        dve.wait_ge(ln_ready, b * NC + (c + 1))
                        last = dve.tensor_tensor(lnrow[p][:, a:z], lnrow[p][:, a:z], liftrow[:, a:z], ALU.min)
                        last.then_inc(min_done, 1)
                        dve.wait_ge(part_filled, b * NC + (c + 1 + NC))
                        dve.wait_ge(part_added, b * NC + (c + 2))
                        k = (c + p) % 2
                        dve.tensor_tensor(sums[:, a:z], sums[:, a:z], acc[k][:, 0:z - a], ALU.add).then_inc(part_added, 1)
                    dve.tensor_reduce(G["deg"][:, bass.ds(b, 1)], deg_parts[p][:, :], AX.X, ALU.add).then_inc(deg_done, 1)
                    dve.wait_ge(diag_ready, b + 1)
                    dve.tensor_reduce(G["selfc"][:, bass.ds(b, 1)], dtile[:, :], AX.X, ALU.add).then_inc(diag_read, 1)
                pairs_of_blocks(dve, step)

            @block.tensor
            def _(pe):
                turns, rounds = start(pe)
                pe.sem_inc(group_done, 2)
                pe.sem_inc(blk_used, 2)
                pe.sem_inc(part_filled, NC)

                def step(b, p, i2):
                    def body(pair, it):
                        for k in range(2):
                            pe.wait_ge(hot_key_ready, 2 * it + (k + 1))
                            pe.wait_ge(added, 2 * it + (k + 1))
                            for i in (2 * k, 2 * k + 1):
                                last = pe.matmul(win[k][:, :], hot_place[:, i, :], hot_key[:, i, :],
                                                 start=(i == 2 * k), stop=(i == 2 * k + 1))
                            last.then_inc(group_done, 1)
                    over_pairs(pe, b, turns, rounds, body)
                    pe.wait_ge(blk_full, b + 1)
                    part = blk[p][:, WN:WN + N].rearrange("p (d t) -> p d t", t=NT)
                    def sum_chunk(c):
                        a, z = CHUNKS[c]
                        pe.wait_ge(bank_read, b * NC + (c + 3))
                        pe.wait_ge(part_added, b * NC + (c + 1))
                        pe.matmul(acc[(c + p) % 2][:, 0:z - a], h_tile[p][:, :], crow[:, a:z],
                                  start=True, stop=True).then_inc(part_filled, 1)
                    pe.wait_ge(h_staged, b + 1)
                    for c, (a, z) in enumerate(CHUNKS):
                        pe.wait_ge(bank_read, b * NC + (c + 1))
                        k = (c + p) % 2
                        for j in range((z - a) // T):
                            last = pe.transpose(turn[k][:, j * T:(j + 1) * T], part[:, :, a // T + j], ident[0:T, 0:T])
                        last.then_inc(turn_ready, 1)
                        if c:
                            sum_chunk(c - 1)
                    pe.wait_ge(turn_ready, b * NC + NC)
                    pe.sem_inc(blk_used, 1)
                    sum_chunk(NC - 1)
                pairs_of_blocks(pe, step)

            @block.scalar
            def _(act):
                act.sem_inc(bank_read, 2)

                def step(b, p, i2):
                    act.wait_ge(bias_out[p], 16 * i2 + 16)
                    act.wait_ge(deg_done, b + 1)
                    for c, (a, z) in enumerate(CHUNKS):
                        k = (c + p) % 2
                        act.wait_ge(turn_ready, b * NC + (c + 1))
                        if c == 0:
                            act.wait_ge(min_done, b * NC)
                        act.activation(lnrow[p][:, a:z], turn[k][:, 0:z - a], ACT.Ln, bias=G["tiny"][0:T, :]).then_inc(ln_in, 1)
                        act.wait_ge(part_filled, b * NC + (c + 1))
                        act.activation(crow[:, a:z], turn[k][:, 0:z - a], ACT.Copy,
                                       accum_out=deg_parts[p][:, c:c + 1]).then_inc(bank_read, 1)
                        act.wait_ge(ln_in, b * NC + (c + 1))
                        act.activation(liftrow[:, a:z], lnrow[p][:, a:z], ACT.Identity, scale=1e28,
                                       bias=G["lift"][0:T, :]).then_inc(ln_ready, 1)
                pairs_of_blocks(act, step)


class Banks:
    def __init__(self, tiles, filled, read, stages):
        self.tiles, self.filled, self.read = tiles, filled, read
        self.readers, self.first = [], {}
        for name, n, reader in stages:
            self.first[name] = len(self.readers)
            self.readers += [reader] * n

    def fill(self, pe, name, i):
        q = self.first[name] + i
        before = q - len(self.tiles)
        if before >= 0:
            who = self.readers[before]
            pe.wait_ge(self.read[who], self.readers[:before + 1].count(who))
        return self.tiles[q % len(self.tiles)]

    def full(self, eng, name, i):
        q = self.first[name] + i
        eng.wait_ge(self.filled, q + 1)
        return self.tiles[q % len(self.tiles)]

    def done(self, eng, name, n=None):
        at = self.first[name]
        who = self.readers[at]
        n = n or next((k for k in range(at, len(self.readers) + 1)
                       if k in self.first.values() and k > at or k == len(self.readers))) - at
        eng.wait_ge(self.read[who], self.readers[:at + n].count(who))


def bank_set(nc, ctx, name, stages, count=4):
    tiles = [ctx.enter_context(nc.psum_tensor(f"{name}_bank{k}", [128, 512], FP32)) for k in range(count)]
    filled = ctx.enter_context(nc.semaphore(f"{name}_filled"))
    read = {who: ctx.enter_context(nc.semaphore(f"{name}_read_{who}")) for who in ("act", "dve")}
    return Banks(tiles, filled, read, stages)


def tiles_of(c):
    a, z = CHUNKS[c]
    return range(a // T, z // T)


def pe_turn(pe, banks, name, src, width, ident):
    for c in range(NC):
        bank = banks.fill(pe, name, c)
        for j, t in enumerate(tiles_of(c)):
            last = pe.transpose(bank[0:width, j * T:(j + 1) * T], src[:, t, 0:width], ident[0:T, 0:T])
        last.then_inc(banks.filled, 1)


def pe_columns(pe, banks, name, weight, src):
    for c, (a, z) in enumerate(CHUNKS):
        bank = banks.fill(pe, name, c)
        pe.matmul(bank[0:weight.shape[1], 0:z - a], weight, src[:, a:z], start=True, stop=True).then_inc(banks.filled, 1)


def pe_rows(pe, banks, name, cols, weights):
    width = weights[0].shape[1]
    for c in range(NC):
        bank = banks.fill(pe, name, c)
        for j, t in enumerate(tiles_of(c)):
            for k, (col, w) in enumerate(zip(cols, weights)):
                last = pe.matmul(bank[0:T, j * width:(j + 1) * width], col[:, t * T:(t + 1) * T], w,
                                 start=(k == 0), stop=(k == len(cols) - 1))
        last.then_inc(banks.filled, 1)


def act_columns(act, banks, name, out, rows=128, func=None, bias=None, scale=1.0):
    for c, (a, z) in enumerate(CHUNKS):
        bank = banks.full(act, name, c)
        if bias is None:
            last = act.activation(out[:, a:z], bank[0:rows, 0:z - a], func or ACT.Copy, scale=scale)
        else:
            last = act.activation(out[:, a:z], bank[0:rows, 0:z - a], func or ACT.Identity, bias=bias, scale=scale)
        last.then_inc(banks.read["act"], 1)


def rows_view(bank, c, width):
    n = len(tiles_of(c))
    return bank[0:T, 0:n * width].rearrange("p (t d) -> p t d", d=width)


def layers_0_1(nc, G):
    HID = 16
    with ExitStack() as ctx:
        sb = lambda name, shape, dt=FP32: ctx.enter_context(nc.sbuf_tensor(name, shape, dt))
        ps = lambda name, shape, dt=FP32: ctx.enter_context(nc.psum_tensor(name, shape, dt))
        sem = lambda name: ctx.enter_context(nc.semaphore(name))
        x, h, agg, ident = G["x"], G["h"], G["agg"], G["ident"]
        cols = sb("cols0", [128, N])
        hid = [sb(f"hid{j}", [128, N]) for j in range(2)]
        work = sb("work0", [T, NT, D])
        stat = sb("stat0", [T, 2, NT])
        small = sb("small0", [T, 3, NT])
        w1 = sb("w1_0", [D, 2 * D])
        w2 = sb("w2_0", [128, 2, D])
        b1 = sb("b1_0", [128, 2])
        b2 = sb("b2_0", [T, D])
        cw1 = sb("cw1", [D, HID])
        cb1 = sb("cb1", [T, HID])
        cw2 = sb("cw2", [HID, D])
        cb2 = sb("cb2", [T, D])
        u = sb("u", [T, NT, HID])
        conv = sb("conv", [T, NT, HID])
        vcols = sb("vcols", [HID, N])
        counts = [sb(f"counts{p}", [T, N]) for p in range(2)]
        sum_ps = [ps(f"sum_ps{p}", [T, HID]) for p in range(2)]
        banks = bank_set(nc, ctx, "l01", [
            ("agg", NC, "dve"), ("hid0", NC, "act"), ("hid1", NC, "act"), ("mlp", NC, "dve"),
            ("h1", NC, "act"), ("u", 1, "dve"), ("v", NC, "act"), ("y", NC, "dve")])
        weights_in = sem("weights_in0")
        dve_done = sem("l01_dve_done")
        agg_ready = sem("l0_sum_ready")
        h_ready = sem("l1_h_ready")
        u_ready = sem("u_ready")
        v_ready = sem("v_ready")
        var_ready = [sem(f"l01_var{k}") for k in range(2)]
        root_ready = [sem(f"l01_root{k}") for k in range(2)]
        deg_ready = sem("deg_ready")
        deg_root = sem("deg_root")
        counts_in = [sem(f"counts_in{p}") for p in range(2)]
        sum_ready = sem("sum_ready")
        sum_read = sem("sum_read")
        soft_in = sem("soft_in")
        soft_out = sem("soft_out")
        with nc.Block() as block:
            @block.sync
            def _(sp):
                for dst, src in (
                        (w1[:, :], G["L0_gnn_W1"]), (w2[:, :, :], G["L0_gnn_W2"].rearrange("(j k) d -> k j d", j=2)),
                        (b1[:, :], G["L0_gnn_b1"].rearrange("(j k) -> k j", j=2)),
                        (b2[:, :], G["L0_gnn_b2"].unsqueeze(0).broadcast_to([T, D])),
                        (cw1[:, :], G["L1_gnn_W1"]), (cw2[:, :], G["L1_gnn_W2"]),
                        (cb1[:, :], G["L1_gnn_b1"].unsqueeze(0).broadcast_to([T, HID])),
                        (cb2[:, :], G["L1_gnn_b2"].unsqueeze(0).broadcast_to([T, D]))):
                    with nc.allow_non_contiguous_dma(reason="small weights"):
                        sp.dma_start(dst, src).then_inc(weights_in, 16)
                for r in range(2):
                    sp.wait_ge(sum_ready, NT * r)
                    sp.dma_start(counts[0][:, :], G["counts_dram"][0, :, :]).then_inc(counts_in[0], 16)
                    sp.dma_start(counts[1][:, :], G["counts_dram"][1, :, :]).then_inc(counts_in[1], 16)
                    with sp.Fori(0, NT // 2 - 1) as i:
                        for p in range(2):
                            sp.wait_ge(sum_ready, NT * r + 2 * i + (p + 1))
                            sp.dma_start(counts[p][:, :], G["counts_dram"][2 * i + (p + 2), :, :]).then_inc(counts_in[p], 16)
                    sp.wait_ge(sum_ready, NT * r + NT - 2)
                    sp.dma_start(counts[0][:, :], G["counts_dram"][NT - 1, :, :]).then_inc(counts_in[0], 16)

            @block.tensor
            def _(pe):
                pe.wait_ge(weights_in, 16 * 8)
                pe.wait_ge(agg_ready, 1)
                pe_turn(pe, banks, "agg", work, D, ident)
                banks.done(pe, "agg")
                for j in range(2):
                    pe_columns(pe, banks, f"hid{j}", w1[:, j * D:(j + 1) * D], cols)
                banks.done(pe, "hid1")
                pe_rows(pe, banks, "mlp", hid, [w2[:, j, :] for j in range(2)])
                pe.wait_ge(h_ready, 1)
                pe_turn(pe, banks, "h1", h, D, ident)
                banks.done(pe, "h1")
                bank = banks.fill(pe, "u", 0)
                for t in range(NT):
                    last = pe.matmul(bank[0:T, t * HID:(t + 1) * HID], cols[:, t * T:(t + 1) * T], cw1[:, :],
                                     start=True, stop=True)
                last.then_inc(banks.filled, 1)
                for r in range(2):
                    pe.wait_ge(u_ready, r + 1)

                    def step(b, p, i2):
                        done = (NT + 1 - p) // 2 * r
                        k = (p + r) % 2
                        pe.wait_ge(counts_in[p], 16 * i2 + 16 * (done + 1))
                        pe.wait_ge(sum_read, NT * r + b + 1)
                        part = counts[p][:, :].rearrange("s (d t) -> s d t", t=NT)
                        for t in range(NT):
                            last = pe.matmul(sum_ps[k][:, :], part[:, :, t], u[:, t, :], start=(t == 0), stop=(t == NT - 1))
                        last.then_inc(sum_ready, 1)
                    pairs_of_blocks(pe, step)
                pe.wait_ge(v_ready, 1)
                pe_turn(pe, banks, "v", conv, HID, ident)
                banks.done(pe, "v")
                pe_rows(pe, banks, "y", [vcols], [cw2[:, :]])

            @block.scalar
            def _(act):
                act.sem_inc(sum_read, 2)
                act.wait_ge(deg_ready, 1)
                act.activation(G["dinv"][:, :], G["dinv"][:, :], ACT.Sqrt).then_inc(deg_root, 1)
                for j in range(2):
                    act_columns(act, banks, f"hid{j}", hid[j], func=ACT.Relu, bias=b1[:, j:j + 1])
                roots(act, stat, var_ready[0], root_ready[0])
                act_columns(act, banks, "h1", cols)
                for r in range(2):
                    def step(b, p, i2):
                        act.wait_ge(sum_ready, NT * r + b + 1)
                        act.activation(conv[:, bass.ds(b, 1), :], sum_ps[(p + r) % 2][:, :].unsqueeze(1), ACT.Copy).then_inc(sum_read, 1)
                    pairs_of_blocks(act, step)
                act_columns(act, banks, "v", vcols, rows=HID)
                act.wait_ge(soft_in, 1)
                act.activation(work[:, :, :], work[:, :, :], ACT.Exp).then_inc(soft_out, 1)
                act.wait_ge(soft_in, 2)
                act.activation(small[:, 1, :], small[:, 1, :], ACT.Ln).then_inc(soft_out, 1)
                roots(act, stat, var_ready[1], root_ready[1])

            @block.vector
            def _(dve):
                m = Marks(dve_done)
                each = lambda v, n: v.unsqueeze(2).broadcast_to([T, NT, n])
                every = lambda v, n: v.unsqueeze(1).broadcast_to([T, NT, n])
                deg, coef = G["deg"][:, :], small[:, 0, :]
                chain(dve, m, dve.tensor_scalar(G["has_in"][:, :], deg, 0.0, None, ALU.is_gt))
                dve.tensor_scalar(G["dinv"][:, :], deg, 1.0, None, ALU.add).then_inc(deg_ready, 1)
                chain(dve, m, dve.tensor_scalar(coef, G["selfc"][:, :], -1.0, 1.0, ALU.mult, ALU.add))
                dve.tensor_tensor(work[:, :, :], h[:, :, :], each(coef, D), ALU.mult).then_inc(agg_ready, 1)
                for c, (a, z) in enumerate(CHUNKS):
                    bank = banks.full(dve, "agg", c)
                    dve.tensor_tensor(cols[:, a:z], agg[:, a:z], bank[:, 0:z - a], ALU.add).then_inc(banks.read["dve"], 1)
                dve.wait_ge(deg_root, 1)
                chain(dve, m, dve.reciprocal(G["dinv"][:, :], G["dinv"][:, :]))
                dve.wait_ge(weights_in, 16 * 8)
                chain(dve, m, dve.tensor_tensor(x[:, :, :], x[:, :, :], every(b2[:, :], D), ALU.add))
                for c in range(NC):
                    ts = tiles_of(c)
                    bank = banks.full(dve, "mlp", c)
                    here = x[:, ts[0]:ts[-1] + 1, :]
                    dve.tensor_tensor(here, here, rows_view(bank, c, D), ALU.add).then_inc(banks.read["dve"], 1)
                banks.done(dve, "mlp")
                layer_norm_relu(dve, m, x[:, :, :], h[:, :, :], work[:, :, :], stat, var_ready[0], root_ready[0])
                dve.sem_inc(h_ready, 1)
                bank = banks.full(dve, "u", 0)
                dve.tensor_tensor(u[:, :, :], bank[0:T, 0:NT * HID].rearrange("p (t d) -> p t d", d=HID),
                                  each(G["dinv"][:, :], HID), ALU.mult).then_inc(banks.read["dve"], 1)
                banks.done(dve, "u", 1)
                dve.sem_inc(u_ready, 1)
                dve.wait_ge(sum_read, 2 + NT)
                chain(dve, m, dve.tensor_tensor(conv[:, :, :], conv[:, :, :], u[:, :, :], ALU.add))
                chain(dve, m, dve.tensor_tensor(conv[:, :, :], conv[:, :, :], each(G["dinv"][:, :], HID), ALU.mult))
                chain(dve, m, dve.tensor_tensor(conv[:, :, :], conv[:, :, :], every(cb1[:, :], HID), ALU.add))
                chain(dve, m, dve.tensor_scalar(conv[:, :, :], conv[:, :, :], 0.0, None, ALU.max))
                chain(dve, m, dve.tensor_tensor(u[:, :, :], conv[:, :, :], each(G["dinv"][:, :], HID), ALU.mult))
                dve.sem_inc(u_ready, 1)
                dve.wait_ge(sum_read, 2 + 2 * NT)
                chain(dve, m, dve.tensor_tensor(conv[:, :, :], conv[:, :, :], u[:, :, :], ALU.add))
                dve.tensor_tensor(conv[:, :, :], conv[:, :, :], each(G["dinv"][:, :], HID), ALU.mult).then_inc(v_ready, 1)
                y = agg[0:T, 0:NT * D].rearrange("p (t d) -> p t d", d=D)
                for c in range(NC):
                    ts = tiles_of(c)
                    bank = banks.full(dve, "y", c)
                    dve.tensor_tensor(y[:, ts[0]:ts[-1] + 1, :], rows_view(bank, c, D),
                                      cb2[:, :].unsqueeze(1).broadcast_to([T, len(ts), D]), ALU.add).then_inc(banks.read["dve"], 1)
                banks.done(dve, "y")
                big, total = small[:, 0, :], small[:, 1, :]
                chain(dve, m, dve.tensor_reduce(big, y, AX.X, ALU.max))
                chain(dve, m, dve.tensor_tensor(y, y, each(big, D), ALU.subtract))
                dve.tensor_copy(work[:, :, :], y).then_inc(soft_in, 1)
                dve.wait_ge(soft_out, 1)
                dve.tensor_reduce(total, work[:, :, :], AX.X, ALU.add).then_inc(soft_in, 1)
                chain(dve, m, dve.tensor_tensor(x[:, :, :], x[:, :, :], y, ALU.add))
                dve.wait_ge(soft_out, 2)
                chain(dve, m, dve.tensor_tensor(x[:, :, :], x[:, :, :], each(total, D), ALU.subtract))
                layer_norm_relu(dve, m, x[:, :, :], h[:, :, :], work[:, :, :], stat, var_ready[1], root_ready[1])


ACT_COPIES = {"gat": (1, 4), "attention": (1, 3, 5)}


class Turned:
    def __init__(self, nbanks, ready, copied, by_act):
        self.nbanks, self.ready, self.copied = nbanks, ready, copied
        self.who = ["act" if c in by_act else "dve" for c in range(NC)]

    def credit(self, eng, who):
        eng.sem_inc(self.copied[who], self.who.count(who))

    def count(self, unit, c):
        who = self.who[c]
        return unit * self.who.count(who) + (self.who[:c + 1].count(who) + self.who.count(who))

    def wait_free(self, pe, unit, c):
        if c >= self.nbanks:
            pe.wait_ge(self.copied[self.who[c - self.nbanks]], self.count(unit, c - self.nbanks))
        else:
            before = max(k for k in range(NC) if k % self.nbanks == c)
            who = self.who[before]
            pe.wait_ge(self.copied[who], self.count(unit, before) - self.who.count(who))

    def wait_copied(self, pe, unit, c):
        pe.wait_ge(self.copied[self.who[c]], self.count(unit, c))

    def copy(self, eng, who, unit, c, bank, out):
        a, z = CHUNKS[c]
        eng.wait_ge(self.ready, unit * NC + (c + 1))
        if who == "act":
            ins = eng.activation(out[:, 0:z - a], bank[:, 0:z - a], ACT.Copy)
        else:
            ins = eng.tensor_copy(out[:, 0:z - a], bank[:, 0:z - a])
        ins.then_inc(self.copied[who], 1)


def graph_attention(nc, G):
    HEADS, CH, SLOPE, EPS = 4, 32, 0.2, 1e-5
    HW = CH + 1
    UNITS = NT * HEADS
    with ExitStack() as ctx:
        sem = lambda name: ctx.enter_context(nc.semaphore(name))
        sbo = lambda name, shape, dt=FP32: ctx.enter_context(nc.sbuf_tensor(name, shape, dt))
        x, h, ident = G["x"], G["h"], G["ident"]
        res = sbo("res", [T, NT, D])
        vals = G["h_mem"][:, :].rearrange("p (t h w) -> p t h w", t=NT, h=HEADS)
        a_row = sbo("a_row", [T, HEADS, N])
        a_own = sbo("a_own", [T, NT, 2 * HEADS])
        logit_own = sbo("logit_own", [T, NT, HEADS])
        a_up = sbo("a_up", [T, NT, HEADS])
        neg_max = sbo("neg_max", [T, NT, HEADS])
        sums = G["agg"][0:T, :].rearrange("p (t h w) -> p t h w", t=NT, h=HEADS)
        with ExitStack() as pre:
            sb = lambda name, shape, dt=FP32: pre.enter_context(nc.sbuf_tensor(name, shape, dt))
            cols = sb("cols2", [128, N])
            vcols = sb("vcols2", [128, N])
            w = sb("w2", [D, D])
            wres = sb("wres", [D, D])
            att = sb("att", [D, 2 * HEADS])
            att_wide = sb("att_wide", [D, HEADS, T])
            banks = bank_set(nc, pre, "l2pre", [
                ("h", NC, "act"), ("vcols", NC, "act"), ("vals", NC, "dve"), ("res", NC, "dve")] +
                [(f"row{k}", NC, "act") for k in range(HEADS)] + [("own", 1, "dve")])
            weights_in = sem("l2_weights_in")
            att_zero = sem("att_zero")
            ones_set = sem("ones_set")
            att_made = sem("att_made")
            pre_dve = sem("l2pre_dve")
            with nc.Block() as block:
                @block.sync
                def _(sp):
                    sp.dma_start(w[:, :], G["L2_gnn_W"]).then_inc(weights_in, 16)
                    sp.dma_start(wres[:, :], G["L2_gnn_W_res"]).then_inc(weights_in, 16)
                    sp.wait_ge(att_zero, 1)
                    for k, name in enumerate(("L2_gnn_att_src", "L2_gnn_att_dst")):
                        for j in range(HEADS):
                            with nc.allow_non_contiguous_dma(reason="small weights"):
                                sp.dma_start(att[j * CH:(j + 1) * CH, k * HEADS + j:k * HEADS + j + 1],
                                             G[name][j:j + 1, :].rearrange("a c -> c a")).then_inc(weights_in, 16)

                @block.gpsimd
                def _(pool):
                    pool.memset(att[:, :], 0.0).then_inc(att_zero, 1)
                    banks.done(pool, "h")
                    pool.memset(vals[:, :, :, CH:HW], 1.0).then_inc(ones_set, 1)

                @block.tensor
                def _(pe):
                    pe_turn(pe, banks, "h", h, D, ident)
                    banks.done(pe, "h")
                    pe.wait_ge(weights_in, 160)
                    pe_columns(pe, banks, "vcols", w[:, :], cols)
                    pe_rows(pe, banks, "vals", [cols], [w[:, :]])
                    pe_rows(pe, banks, "res", [cols], [wres[:, :]])
                    banks.done(pe, "vcols")
                    pe.wait_ge(att_made, 1)
                    for k in range(HEADS):
                        pe_columns(pe, banks, f"row{k}", att_wide[:, k, :], vcols)
                    bank = banks.fill(pe, "own", 0)
                    for t in range(NT):
                        last = pe.matmul(bank[0:T, 8 * t:8 * t + 8], vcols[:, t * T:(t + 1) * T], att[:, :], start=True, stop=True)
                    last.then_inc(banks.filled, 1)

                @block.scalar
                def _(act):
                    act_columns(act, banks, "h", cols)
                    act_columns(act, banks, "vcols", vcols)
                    for k in range(HEADS):
                        act_columns(act, banks, f"row{k}", a_row[:, k, :], rows=T, scale=SLOPE)

                @block.vector
                def _(dve):
                    m = Marks(pre_dve)
                    dve.wait_ge(weights_in, 160)
                    dve.tensor_copy(att_wide[:, :, :], att[:, 0:HEADS].unsqueeze(2).broadcast_to([D, HEADS, T])).then_inc(att_made, 1)
                    for name in ("vals", "res"):
                        for c in range(NC):
                            ts = tiles_of(c)
                            bank = banks.full(dve, name, c)
                            if name == "res":
                                dve.tensor_copy(res[:, ts[0]:ts[-1] + 1, :], rows_view(bank, c, D)).then_inc(banks.read["dve"], 1)
                            else:
                                dve.tensor_copy(vals[:, ts[0]:ts[-1] + 1, :, 0:CH],
                                                bank[0:T, 0:len(ts) * D].rearrange("p (t h w) -> p t h w", h=HEADS, w=CH)
                                                ).then_inc(banks.read["dve"], 1)
                    bank = banks.full(dve, "own", 0)
                    dve.tensor_copy(a_own[:, :, :], bank[0:T, 0:NT * 8].rearrange("p (t k) -> p t k", k=8)).then_inc(banks.read["dve"], 1)
                    banks.done(dve, "own", 1)
                    chain(dve, m, dve.tensor_tensor(logit_own[:, :, :], a_own[:, :, 0:HEADS], a_own[:, :, HEADS:], ALU.add))
                    chain(dve, m, dve.scalar_tensor_tensor(out=logit_own[:, :, :], in0=logit_own[:, :, :], scalar=SLOPE,
                                                           in1=logit_own[:, :, :], op0=ALU.mult, op1=ALU.max))
                    chain(dve, m, dve.scalar_tensor_tensor(out=logit_own[:, :, :], in0=a_own[:, :, HEADS:], scalar=-SLOPE,
                                                           in1=logit_own[:, :, :], op0=ALU.mult, op1=ALU.add))
                    chain(dve, m, dve.tensor_scalar(a_up[:, :, :], a_own[:, :, HEADS:], 1.0 - SLOPE, None, ALU.mult))

        with ExitStack() as loop:
            sb = lambda name, shape, dt=FP32: loop.enter_context(nc.sbuf_tensor(name, shape, dt))
            ps = lambda name, shape, dt=FP32: loop.enter_context(nc.psum_tensor(name, shape, dt))
            row = [sb(f"row{k}", [T, N]) for k in range(HEADS)]
            up = sb("up", [T, N])
            bias = [sb(f"bias{p}", [T, N]) for p in range(2)]
            wcol = [sb(f"wcol{k}", [T, C4]) for k in range(4)]
            own = [sb(f"own{p}", [T, HEADS]) for p in range(2)]
            top = sb("top", [T, HEADS])
            bank = [ps(f"turned{k}", [T, C4]) for k in range(4)]
            sum_ps = [ps(f"gat_sum{k}", [T, HW]) for k in range(2)]
            bias_in = [sem(f"bias_in{p}") for p in range(2)]
            bias_read = sem("bias_read")
            base_made = sem("base_made")
            up_made = sem("up_made")
            top_done = sem("top_done")
            max_done = sem("max_done")
            exp_done = sem("exp_done")
            row_used = sem("row_used")
            own_staged = sem("own_staged")
            gat_sum = sem("gat_sum_ready")
            sum_read = sem("gat_sum_read")
            turned = Turned(4, sem("gat_turned"), {w: sem(f"gat_copied_{w}") for w in ("act", "dve")}, ACT_COPIES["gat"])
            HALF = CHUNKS[2][1]

            with nc.Block() as block:
                @block.sync
                def _(sp):
                    def step(b, p, i2):
                        sp.wait_ge(bias_read, b + 1)
                        sp.dma_start(bias[p][:, :], G["bias_dram"][b, :, :]).then_inc(bias_in[p], 16)
                    pairs_of_blocks(sp, step)

                @block.gpsimd
                def _(pool):
                    def step(b, p, i2):
                        pool.wait_ge(max_done, HEADS * b)
                        pool.tensor_copy(own[p][:, :].unsqueeze(1), logit_own[:, bass.ds(b, 1), :]).then_inc(own_staged, 1)
                        pool.wait_ge(bias_in[p], 16 * i2 + 16)
                        for k in range(HEADS):
                            pool.wait_ge(row_used, HEADS * b + (k + 1))
                            pool.tensor_tensor(row[k][:, :], a_row[:, k, :], bias[p][:, :], ALU.add).then_inc(base_made, 1)
                        pool.wait_ge(base_made, HEADS * b + HEADS)
                        pool.sem_inc(bias_read, 1)
                    pool.sem_inc(bias_read, 2)
                    pairs_of_blocks(pool, step)

                @block.scalar
                def _(act):
                    turned.credit(act, "act")

                    def logits(b, k):
                        act.wait_ge(top_done, HEADS * b + k)
                        act.activation(up[:, :], a_row[:, k, :], ACT.Relu, scale=(1.0 - SLOPE) / SLOPE,
                                       bias=a_up[:, bass.ds(b, 1), k:k + 1].rearrange("p a k -> p (a k)")
                                       ).then_inc(up_made, 1)

                    def unit(b, k):
                        u = HEADS * b + k
                        act.wait_ge(max_done, u + 1)
                        for a, z in ((0, HALF), (HALF, N)):
                            act.activation(row[k][:, a:z], row[k][:, a:z], ACT.Exp,
                                           bias=neg_max[:, bass.ds(b, 1), k:k + 1].rearrange("p a k -> p (a k)")
                                           ).then_inc(exp_done, 1)

                    def copies(b, k):
                        for c in ACT_COPIES["gat"]:
                            turned.copy(act, "act", HEADS * b + k, c, bank[c % 4], wcol[c % 4])

                    logits(0, 0)

                    def block_of(b, last):
                        for k in range(HEADS):
                            if k + 1 < HEADS:
                                logits(b, k + 1)
                            elif not last:
                                logits(b + 1, 0)
                            unit(b, k)
                            copies(b, k)
                    with act.Fori(0, NT - 1) as b:
                        block_of(b, False)
                    block_of(NT - 1, True)

                @block.vector
                def _(dve):
                    turned.credit(dve, "dve")
                    dve.sem_inc(sum_read, 2)

                    def maximum(b, p, i2, k):
                        u = HEADS * b + k
                        if k == 0:
                            dve.wait_ge(own_staged, b + 1)
                        dve.wait_ge(base_made, u + 1)
                        dve.wait_ge(up_made, u + 1)
                        dve.sem_inc(G["passed"], 1)
                        dve.tensor_tensor_reduce(out=row[k][:, :], in0=row[k][:, :], in1=up[:, :], scale=1.0,
                                                 scalar=own[p][:, k:k + 1], op0=ALU.add, op1=ALU.max,
                                                 accum_out=top[:, k:k + 1]).then_inc(top_done, 1)
                        dve.wait_ge(top_done, u + 1)
                        dve.tensor_scalar(neg_max[:, bass.ds(b, 1), k:k + 1].rearrange("p a k -> p (a k)"), top[:, k:k + 1],
                                          -1.0, None, ALU.mult).then_inc(max_done, 1)

                    def copies(b, k):
                        u = HEADS * b + k
                        for c in range(NC):
                            if c not in ACT_COPIES["gat"]:
                                turned.copy(dve, "dve", u, c, bank[c % 4], wcol[c % 4])
                        dve.wait_ge(gat_sum, u + 1)
                        dve.tensor_copy(sums[:, bass.ds(b, 1), k, :], sum_ps[k % 2][:, :].unsqueeze(1)).then_inc(sum_read, 1)

                    maximum(0, 0, 0, 0)

                    def step(b, p, i2, last=False):
                        for k in range(HEADS):
                            if k + 1 < HEADS:
                                maximum(b, p, i2, k + 1)
                            elif not last:
                                maximum(b + 1, 1 - p, i2 + p, 0)
                            copies(b, k)
                    with dve.Fori(0, NT // 2) as i:
                        step(2 * i, 0, i)
                        step(2 * i + 1, 1, i)
                    step(NT - 1, 0, NT // 2, last=True)

                @block.tensor
                def _(pe):
                    pe.sem_inc(row_used, HEADS)

                    def weigh(b, k, c):
                        u = HEADS * b + k
                        if c == 0:
                            pe.wait_ge(sum_read, u + 1)
                        turned.wait_copied(pe, u, c)
                        for j, t in enumerate(tiles_of(c)):
                            last = pe.matmul(sum_ps[k % 2][:, :], wcol[c % 4][:, j * T:(j + 1) * T], vals[:, t, k, :],
                                             start=(t == 0), stop=(t == NT - 1))
                        if c == NC - 1:
                            last.then_inc(gat_sum, 1)

                    with pe.Fori(0, NT) as b:
                        for k in range(HEADS):
                            u = HEADS * b + k
                            for c in range(NC):
                                if CHUNKS[c][0] in (0, HALF):
                                    pe.wait_ge(exp_done, 2 * u + (1 if c == 0 else 2))
                                turned.wait_free(pe, u, c)
                                for j, t in enumerate(tiles_of(c)):
                                    last = pe.transpose(bank[c % 4][:, j * T:(j + 1) * T], row[k][:, t * T:(t + 1) * T], ident[0:T, 0:T])
                                last.then_inc(turned.ready, 1)
                                if c:
                                    weigh(b, k, c - 1)
                            pe.wait_ge(turned.ready, u * NC + NC)
                            pe.sem_inc(row_used, 1)
                            weigh(b, k, NC - 1)

        with ExitStack() as post:
            sb = lambda name, shape, dt=FP32: post.enter_context(nc.sbuf_tensor(name, shape, dt))
            work = sb("work2", [T, NT, D])
            stat = sb("stat2", [T, 2, NT])
            e_own = sb("e_own", [T, NT, HEADS])
            total = sb("total", [T, NT, HEADS])
            rows = sb("rows2", [T, 5, D])
            rows_in = sem("l2_rows_in")
            own_made = sem("own_made")
            own_exp = sem("own_exp")
            root_in, root_out = sem("l2_root_in"), sem("l2_root_out")
            elu_in, elu_out = sem("elu_in"), sem("elu_out")
            post_dve = sem("l2post_dve")
            var_ready, root_ready = sem("l2_var"), sem("l2_root")
            with nc.Block() as block:
                @block.sync
                def _(sp):
                    for k, name in enumerate(("bias", "bn_gamma", "bn_beta", "bn_mean", "bn_var")):
                        sp.dma_start(rows[:, k, :], G[f"L2_gnn_{name}"].unsqueeze(0).broadcast_to([T, D])).then_inc(rows_in, 16)

                @block.scalar
                def _(act):
                    act.wait_ge(own_made, 1)
                    act.activation(e_own[:, :, :], e_own[:, :, :], ACT.Exp).then_inc(own_exp, 1)
                    act.wait_ge(root_in, 1)
                    act.activation(rows[:, 4, :], rows[:, 4, :], ACT.Sqrt).then_inc(root_out, 1)
                    act.wait_ge(elu_in, 1)
                    act.activation(work[:, :, :], work[:, :, :], ACT.Exp).then_inc(elu_out, 1)
                    roots(act, stat, var_ready, root_ready)

                @block.vector
                def _(dve):
                    m = Marks(post_dve)
                    every = lambda k: rows[:, k, :].unsqueeze(1).broadcast_to([T, NT, D])
                    heads = lambda v: v.unsqueeze(3).broadcast_to([T, NT, HEADS, CH])
                    w4 = work[:, :, :].rearrange("p t (h w) -> p t h w", h=HEADS)
                    dve.tensor_tensor(e_own[:, :, :], logit_own[:, :, :], neg_max[:, :, :], ALU.add).then_inc(own_made, 1)
                    dve.wait_ge(rows_in, 80)
                    dve.tensor_scalar(rows[:, 4, :], rows[:, 4, :], EPS, None, ALU.add).then_inc(root_in, 1)
                    dve.wait_ge(own_exp, 1)
                    chain(dve, m, dve.tensor_tensor(total[:, :, :], sums[:, :, :, CH], e_own[:, :, :], ALU.add))
                    chain(dve, m, dve.reciprocal(total[:, :, :], total[:, :, :]))
                    for k in range(HEADS):
                        chain(dve, m, dve.tensor_tensor(w4[:, :, k, :], vals[:, :, k, 0:CH],
                                                        e_own[:, :, k].unsqueeze(2).broadcast_to([T, NT, CH]), ALU.mult))
                        chain(dve, m, dve.tensor_tensor(w4[:, :, k, :], w4[:, :, k, :], sums[:, :, k, 0:CH], ALU.add))
                        chain(dve, m, dve.tensor_tensor(w4[:, :, k, :], w4[:, :, k, :],
                                                        total[:, :, k].unsqueeze(2).broadcast_to([T, NT, CH]), ALU.mult))
                    chain(dve, m, dve.tensor_tensor(work[:, :, :], work[:, :, :], res[:, :, :], ALU.add))
                    chain(dve, m, dve.tensor_tensor(work[:, :, :], work[:, :, :], every(0), ALU.add))
                    chain(dve, m, dve.tensor_tensor(work[:, :, :], work[:, :, :], every(3), ALU.subtract))
                    dve.wait_ge(root_out, 1)
                    chain(dve, m, dve.reciprocal(rows[:, 4, :], rows[:, 4, :]))
                    chain(dve, m, dve.tensor_tensor(rows[:, 1, :], rows[:, 1, :], rows[:, 4, :], ALU.mult))
                    chain(dve, m, dve.tensor_tensor(work[:, :, :], work[:, :, :], every(1), ALU.mult))
                    chain(dve, m, dve.tensor_tensor(work[:, :, :], work[:, :, :], every(2), ALU.add))
                    chain(dve, m, dve.tensor_scalar(res[:, :, :], work[:, :, :], 0.0, -1.0, ALU.max, ALU.add))
                    dve.tensor_scalar(work[:, :, :], work[:, :, :], 0.0, None, ALU.min).then_inc(elu_in, 1)
                    chain(dve, m, dve.tensor_tensor(x[:, :, :], x[:, :, :], res[:, :, :], ALU.add))
                    dve.wait_ge(elu_out, 1)
                    chain(dve, m, dve.tensor_tensor(x[:, :, :], x[:, :, :], work[:, :, :], ALU.add))
                    layer_norm_relu(dve, m, x[:, :, :], h[:, :, :], work[:, :, :], stat, var_ready, root_ready)


def transformer(nc, G):
    LAYERS, EPS = 4, 1e-5
    SCALE = float(1.0 / np.sqrt(D))
    S_BANKS = T_BANKS = 3
    with ExitStack() as ctx:
        sbo = lambda name, shape, dt=FP32: ctx.enter_context(nc.sbuf_tensor(name, shape, dt))
        x, h, ident, msg_mem = G["x"], G["h"], G["ident"], G["agg"]
        msg = msg_mem[0:T, 0:NT * D].rearrange("p (t d) -> p t d", d=D)
        cols = sbo("cols3", [128, N])
        work = sbo("work3", [T, NT, D])
        stat = sbo("stat3", [T, 2, NT])

        def every(v):
            return v.unsqueeze(1).broadcast_to([T, NT, D])

        def project(tag, w_src, b_src, into_x):
            with ExitStack() as pre:
                w = pre.enter_context(nc.sbuf_tensor(f"w_{tag}", [D, D], FP32))
                b = pre.enter_context(nc.sbuf_tensor(f"b_{tag}", [T, D], FP32))
                banks = bank_set(nc, pre, tag, [("h", NC, "act"), ("out", NC, "dve")])
                loaded = pre.enter_context(nc.semaphore(f"{tag}_loaded"))
                added = pre.enter_context(nc.semaphore(f"{tag}_added"))
                stored = pre.enter_context(nc.semaphore(f"{tag}_stored"))
                with nc.Block() as block:
                    @block.sync
                    def _(sp):
                        sp.dma_start(w[:, :], w_src).then_inc(loaded, 16)
                        sp.dma_start(b[:, :], b_src.unsqueeze(0).broadcast_to([T, D])).then_inc(loaded, 16)
                        if into_x:
                            sp.wait_ge(added, NC)
                            sp.dma_start(G["out"].rearrange("(t p) d -> p t d", p=T), x[:, :, :]).then_inc(stored, 16)
                            sp.wait_ge(stored, 16)

                    @block.tensor
                    def _(pe):
                        pe_turn(pe, banks, "h", h, D, ident)
                        banks.done(pe, "h")
                        pe.wait_ge(loaded, 32)
                        pe_rows(pe, banks, "out", [cols], [w[:, :]])

                    @block.scalar
                    def _(act):
                        act_columns(act, banks, "h", cols)

                    @block.vector
                    def _(dve):
                        dve.wait_ge(loaded, 32)
                        for c in range(NC):
                            ts = tiles_of(c)
                            bank = banks.full(dve, "out", c)
                            wide = b[:, :].unsqueeze(1).broadcast_to([T, len(ts), D])
                            part = slice(ts[0], ts[-1] + 1)
                            if into_x:
                                dve.tensor_tensor(work[:, part, :], rows_view(bank, c, D), wide, ALU.add).then_inc(banks.read["dve"], 1)
                                dve.wait_ge(banks.read["dve"], c + 1)
                                dve.tensor_tensor(x[:, part, :], x[:, part, :], work[:, part, :], ALU.add).then_inc(added, 1)
                            else:
                                dve.tensor_tensor(h[:, part, :], rows_view(bank, c, D), wide, ALU.add).then_inc(banks.read["dve"], 1)

        project("node_in", G["L3_gnn_Wn"], G["L3_gnn_bn"], False)

        with ExitStack() as lctx:
            sb = lambda name, shape, dt=FP32: lctx.enter_context(nc.sbuf_tensor(name, shape, dt))
            w = sb("w3", [D, 4, D])
            bq = sb("bq", [D, 2])
            rows = sb("rows3", [T, 4, D])
            q = sb("q", [D, N])
            k_all = sb("k_all", [D, N])
            vals = sb("vals3", [T, NT, D + 1])
            with nc.Fori(0, LAYERS) as l:
                used = []

                with ExitStack() as pre:
                    banks = bank_set(nc, pre, "qkv", [
                        ("h", NC, "act"), ("q", NC, "act"), ("k", NC, "dve"), ("v", NC, "dve")])
                    loaded = pre.enter_context(nc.semaphore("qkv_loaded"))
                    scaled = pre.enter_context(nc.semaphore("bq_scaled"))
                    used += [banks.filled, *banks.read.values(), loaded, scaled]
                    with nc.Block() as block:
                        @block.sync
                        def _(sp):
                            for j, name in enumerate(("WQ", "WK", "WV", "WO")):
                                sp.dma_start(w[:, j, :], G[f"L3_gnn_{name}"][l, :, :]).then_inc(loaded, 16)
                            for j, name in enumerate(("bQ", "bK")):
                                with nc.allow_non_contiguous_dma(reason="a bias as a column"):
                                    sp.dma_start(bq[:, j:j + 1], G[f"L3_gnn_{name}"][bass.ds(l, 1), :].rearrange("a d -> d a")).then_inc(loaded, 16)
                            for j, name in enumerate(("bV", "bO", "ln_g", "ln_b")):
                                sp.dma_start(rows[:, j, :], G[f"L3_gnn_{name}"][bass.ds(l, 1), :].broadcast_to([T, D])).then_inc(loaded, 16)

                        @block.gpsimd
                        def _(pool):
                            pool.memset(vals[:, :, D:D + 1], 1.0)

                        @block.tensor
                        def _(pe):
                            pe_turn(pe, banks, "h", h, D, ident)
                            banks.done(pe, "h")
                            pe.wait_ge(loaded, 160)
                            pe_columns(pe, banks, "q", w[:, 0, :], cols)
                            pe_columns(pe, banks, "k", w[:, 1, :], cols)
                            pe_rows(pe, banks, "v", [cols], [w[:, 2, :]])

                        @block.scalar
                        def _(act):
                            act_columns(act, banks, "h", cols)
                            act.wait_ge(scaled, 1)
                            act_columns(act, banks, "q", q, bias=bq[:, 0:1], scale=SCALE)

                        @block.vector
                        def _(dve):
                            dve.wait_ge(loaded, 160)
                            dve.tensor_scalar(bq[:, 0:1], bq[:, 0:1], SCALE, None, ALU.mult).then_inc(scaled, 1)
                            for c, (a, z) in enumerate(CHUNKS):
                                bank = banks.full(dve, "k", c)
                                dve.tensor_scalar(k_all[:, a:z], bank[:, 0:z - a], bq[:, 1:2], None, ALU.add).then_inc(banks.read["dve"], 1)
                            for c in range(NC):
                                ts = tiles_of(c)
                                bank = banks.full(dve, "v", c)
                                dve.tensor_tensor(vals[:, ts[0]:ts[-1] + 1, 0:D], rows_view(bank, c, D),
                                                  rows[:, 0, :].unsqueeze(1).broadcast_to([T, len(ts), D]), ALU.add
                                                  ).then_inc(banks.read["dve"], 1)

                with ExitStack() as loop:
                    lsb = lambda name, shape, dt=FP32: loop.enter_context(nc.sbuf_tensor(name, shape, dt))
                    ps = lambda name, shape, dt=FP32: loop.enter_context(nc.psum_tensor(name, shape, dt))

                    def sem(name):
                        s = loop.enter_context(nc.semaphore(name))
                        used.append(s)
                        return s
                    row = [lsb(f"arow{p}", [T, N]) for p in range(2)]
                    bias = [lsb(f"abias{p}", [T, N]) for p in range(2)]
                    wcol = [lsb(f"awcol{k}", [T, C4]) for k in range(T_BANKS)]
                    q_tile = [lsb(f"q_tile{p}", [D, T]) for p in range(2)]
                    top = [lsb(f"atop{p}", [T, NC]) for p in range(2)]
                    neg = [lsb(f"aneg{p}", [T, 1]) for p in range(2)]
                    inv = [lsb(f"ainv{p}", [T, 1]) for p in range(2)]
                    s_ps = [ps(f"scores{k}", [T, C4]) for k in range(S_BANKS)]
                    bank = [ps(f"aturned{k}", [T, C4]) for k in range(T_BANKS)]
                    sum_ps = [ps(f"asum{p}", [T, D + 1]) for p in range(2)]
                    bias_in = [sem(f"abias_in{p}") for p in range(2)]
                    q_staged = sem("q_staged")
                    scores_ready = sem("scores_ready")
                    scores_read = sem("scores_read")
                    max_done = sem("amax_done")
                    exp_done = sem("aexp_done")
                    row_used = sem("arow_used")
                    sum_ready = sem("asum_ready")
                    sum_read = sem("asum_read")
                    inv_done = sem("ainv_done")
                    turned = Turned(T_BANKS, sem("aturned_ready"), {k: sem(f"acopied_{k}") for k in ("act", "dve")},
                                    ACT_COPIES["attention"])

                    with nc.Block() as block:
                        @block.sync
                        def _(sp):
                            def step(b, p, i2):
                                sp.wait_ge(scores_read, b * NC)
                                sp.dma_start(bias[p][:, :], G["bias_dram"][b, :, :]).then_inc(bias_in[p], 16)
                            pairs_of_blocks(sp, step)

                        @block.gpsimd
                        def _(pool):
                            def step(b, p, i2):
                                pool.wait_ge(scores_read, b * NC)
                                pool.tensor_copy(q_tile[p][:, :], q[:, bass.ds(b * T, T)]).then_inc(q_staged, 1)
                            pairs_of_blocks(pool, step)

                        @block.tensor
                        def _(pe):
                            pe.sem_inc(row_used, 2)

                            def scores(b, p, c):
                                a, z = CHUNKS[c]
                                if c == 0:
                                    pe.wait_ge(q_staged, b + 1)
                                before = c - S_BANKS if c >= S_BANKS else max(k for k in range(NC) if k % S_BANKS == c) - NC
                                pe.wait_ge(scores_read, b * NC + (before + 1 + NC))
                                pe.matmul(s_ps[c % S_BANKS][:, 0:z - a], q_tile[p][:, :], k_all[:, a:z],
                                          start=True, stop=True).then_inc(scores_ready, 1)

                            def weigh(b, p, c):
                                if c == 0:
                                    pe.wait_ge(sum_read, b + 1)
                                turned.wait_copied(pe, b, c)
                                for j, t in enumerate(tiles_of(c)):
                                    last = pe.matmul(sum_ps[p][:, :], wcol[c % T_BANKS][:, j * T:(j + 1) * T], vals[:, t, :],
                                                     start=(t == 0), stop=(t == NT - 1))
                                if c == NC - 1:
                                    last.then_inc(sum_ready, 1)

                            def turn(b, p, c):
                                pe.wait_ge(exp_done, b * NC + (c + 1))
                                turned.wait_free(pe, b, c)
                                for j, t in enumerate(tiles_of(c)):
                                    last = pe.transpose(bank[c % T_BANKS][:, j * T:(j + 1) * T], row[p][:, t * T:(t + 1) * T], ident[0:T, 0:T])
                                last.then_inc(turned.ready, 1)

                            def step(b, p, last=False):
                                for c in range(NC):
                                    if not last:
                                        scores(b + 1, 1 - p, c)
                                    turn(b, p, c)
                                    if c:
                                        weigh(b, p, c - 1)
                                pe.wait_ge(turned.ready, b * NC + NC)
                                pe.sem_inc(row_used, 1)
                                weigh(b, p, NC - 1)
                            for c in range(NC):
                                scores(0, 0, c)
                            with pe.Fori(0, NT // 2) as i:
                                step(2 * i, 0)
                                step(2 * i + 1, 1)
                            step(NT - 1, 0, last=True)

                        @block.scalar
                        def _(act):
                            turned.credit(act, "act")

                            def step(b, p, i2):
                                act.wait_ge(max_done, b + 1)
                                for a, z in CHUNKS:
                                    act.activation(row[p][:, a:z], row[p][:, a:z], ACT.Exp, bias=neg[p][:, :]).then_inc(exp_done, 1)
                                for c in ACT_COPIES["attention"]:
                                    turned.copy(act, "act", b, c, bank[c % T_BANKS], wcol[c % T_BANKS])
                            pairs_of_blocks(act, step)

                        @block.vector
                        def _(dve):
                            turned.credit(dve, "dve")
                            dve.sem_inc(scores_read, NC)
                            dve.sem_inc(sum_read, 2)

                            def maximum(b, p, i2, c):
                                a, z = CHUNKS[c]
                                if c == 0:
                                    dve.wait_ge(bias_in[p], 16 * i2 + 16)
                                    dve.wait_ge(row_used, b + 1)
                                dve.wait_ge(scores_ready, b * NC + (c + 1))
                                dve.sem_inc(G["passed"], 1)
                                dve.tensor_tensor_reduce(out=row[p][:, a:z], in0=s_ps[c % S_BANKS][:, 0:z - a], in1=bias[p][:, a:z],
                                                         scale=1.0, scalar=-3.0e38, op0=ALU.add, op1=ALU.max,
                                                         accum_out=top[p][:, c:c + 1]).then_inc(scores_read, 1)
                                if c == NC - 1:
                                    dve.wait_ge(scores_read, b * NC + 2 * NC)
                                    dve.sem_inc(G["passed"], 1)
                                    dve.tensor_reduce(neg[p][:, :], top[p][:, :], AX.X, ALU.max, negate=True).then_inc(max_done, 1)

                            def finish(b, p):
                                dve.wait_ge(sum_ready, b + 1)
                                dve.reciprocal(inv[p][:, :], sum_ps[p][:, D:D + 1]).then_inc(inv_done, 1)
                                dve.wait_ge(inv_done, b + 1)
                                dve.tensor_scalar(msg[:, bass.ds(b, 1), :], sum_ps[p][:, 0:D].unsqueeze(1), inv[p][:, :],
                                                  G["has_in"][:, bass.ds(b, 1)], ALU.mult, ALU.mult).then_inc(sum_read, 1)

                            def step(b, p, i2, last=False):
                                for c in range(NC):
                                    if not last:
                                        maximum(b + 1, 1 - p, i2 + p, c)
                                    if c not in ACT_COPIES["attention"]:
                                        turned.copy(dve, "dve", b, c, bank[c % T_BANKS], wcol[c % T_BANKS])
                                finish(b, p)
                            for c in range(NC):
                                maximum(0, 0, 0, c)
                            with dve.Fori(0, NT // 2) as i:
                                step(2 * i, 0, i)
                                step(2 * i + 1, 1, i)
                            step(NT - 1, 0, NT // 2, last=True)

                with ExitStack() as post:
                    banks = bank_set(nc, post, "attn_out", [("msg", NC, "act"), ("out", NC, "dve")])
                    post_done = post.enter_context(nc.semaphore("l3_post_dve"))
                    var_ready = post.enter_context(nc.semaphore("l3_var"))
                    root_ready = post.enter_context(nc.semaphore("l3_root"))
                    used += [banks.filled, *banks.read.values(), post_done, var_ready, root_ready]
                    with nc.Block() as block:
                        @block.tensor
                        def _(pe):
                            pe_turn(pe, banks, "msg", msg, D, ident)
                            banks.done(pe, "msg")
                            pe_rows(pe, banks, "out", [cols], [w[:, 3, :]])

                        @block.scalar
                        def _(act):
                            act_columns(act, banks, "msg", cols)
                            roots(act, stat, var_ready, root_ready)

                        @block.vector
                        def _(dve):
                            m = Marks(post_done)
                            for c in range(NC):
                                ts = tiles_of(c)
                                bank = banks.full(dve, "out", c)
                                part = slice(ts[0], ts[-1] + 1)
                                dve.tensor_tensor(work[:, part, :], rows_view(bank, c, D), h[:, part, :], ALU.add).then_inc(banks.read["dve"], 1)
                            banks.done(dve, "out")
                            chain(dve, m, dve.tensor_tensor(work[:, :, :], work[:, :, :], every(rows[:, 1, :]), ALU.add))
                            layer_norm(dve, m, work[:, :, :], h[:, :, :], msg, stat, var_ready, root_ready)
                            chain(dve, m, dve.tensor_tensor(h[:, :, :], h[:, :, :], every(rows[:, 2, :]), ALU.mult))
                            chain(dve, m, dve.tensor_tensor(h[:, :, :], h[:, :, :], every(rows[:, 3, :]), ALU.add))
                    with nc.Block() as block:
                        @block.sync
                        def _(sp):
                            for s in {s.num: s for s in used}.values():
                                sp.sem_clear(s)

        project("node_out", G["L3_gnn_Wout"], G["L3_gnn_bout"], True)


INPUTS = ["x", "src", "dst",
          "L0_gnn_W1", "L0_gnn_b1", "L0_gnn_W2", "L0_gnn_b2",
          "L1_gnn_W1", "L1_gnn_b1", "L1_gnn_W2", "L1_gnn_b2",
          "L2_gnn_W", "L2_gnn_att_src", "L2_gnn_att_dst", "L2_gnn_bias", "L2_gnn_W_res",
          "L2_gnn_bn_gamma", "L2_gnn_bn_beta", "L2_gnn_bn_mean", "L2_gnn_bn_var",
          "L3_gnn_Wn", "L3_gnn_bn", "L3_gnn_WQ", "L3_gnn_bQ", "L3_gnn_WK", "L3_gnn_bK",
          "L3_gnn_WV", "L3_gnn_bV", "L3_gnn_WO", "L3_gnn_bO", "L3_gnn_ln_g", "L3_gnn_ln_b",
          "L3_gnn_Wout", "L3_gnn_bout"]


def program(nc, ins, out):
    with ExitStack() as ctx:
        sb = lambda name, shape, dt=FP32: ctx.enter_context(nc.sbuf_tensor(name, shape, dt))
        dram = lambda name, shape, dt=FP32: nc.dram_tensor(name, shape, dt).ap()
        G = dict(ins)
        G["x_in"], G["out"] = ins["x"], out
        G["x"] = sb("x", [T, NT, D])
        G["h_mem"] = sb("h_mem", [T, NT * 132])
        G["h"] = G["h_mem"][:, 0:NT * D].rearrange("p (t d) -> p t d", d=D)
        G["agg"] = sb("agg", [128, NT * 132])
        G["deg"] = sb("deg", [T, NT])
        G["selfc"] = sb("selfc", [T, NT])
        G["ident"] = sb("ident", [128, 128])
        G["dinv"] = sb("dinv", [T, NT])
        G["has_in"] = sb("has_in", [T, NT])
        G["passed"] = ctx.enter_context(nc.semaphore("passed"))
        G["counts_dram"] = dram("counts_dram", [NT, T, N])
        G["bias_dram"] = dram("bias_dram", [NT, T, N])
        with ExitStack() as edges:
            se = lambda name, shape, dt=FP32: edges.enter_context(nc.sbuf_tensor(name, shape, dt))
            G["key"] = se("key", [EP, 4 * NPAIR])
            G["place"] = se("place", [EP, 4 * NPAIR])
            G["gmin"] = se("gmin", [1, 2 * NPAIR])
            G["ranges"] = se("ranges", [1, 3 * NT], I32)
            G["iota_win"] = se("iota_win", [EP, WN], FP16)
            G["iota_t"] = se("iota_t", [EP, 2, T], FP16)
            G["tiny"] = se("tiny", [128, 1])
            G["lift"] = se("lift", [128, 1])
            G["mm_dram"] = dram("mm_dram", [2, 2 * NPAIR])
            G["tab_dram"] = dram("tab_dram", [NT, 3], I32)
            prepare(nc, G)
            build_counts(nc, G)
        layers_0_1(nc, G)
        graph_attention(nc, G)
        transformer(nc, G)


def kernel(**inputs):
    from concourse import bacc
    from concourse.bass_utils import run_bass_kernel_spmd

    nc = bacc.Bacc("TRN2", target_bir_lowering=False, num_devices=1)
    arrays, ins = {}, {}
    for name in INPUTS:
        a = np.ascontiguousarray(inputs[name])
        arrays["in_" + name] = a
        ins[name] = nc.dram_tensor("in_" + name, a.shape, mybir.dt.from_np(a.dtype), kind="ExternalInput").ap()
    out = nc.dram_tensor("out", (N, D), FP32, kind="ExternalOutput").ap()
    program(nc, ins, out)
    return run_bass_kernel_spmd(nc, [arrays], core_ids=[0]).results[0]["out"]
```

```python
from contextlib import ExitStack

import numpy as np

import concourse.bass as bass
from concourse import mybir

FP32, BF16, FP16, I32 = mybir.dt.float32, mybir.dt.bfloat16, mybir.dt.float16, mybir.dt.int32
FP32R = mybir.dt.float32r
ALU = mybir.AluOpType
ACT = mybir.ActivationFunctionType
AX = mybir.AxisListType

N, E, D = 3125, 100000, 128
T = 125
NT = N // T
C4 = 4 * T
NC = (NT + 3) // 4
FULL = NT - 3 * NC
CHUNKS = [(T * (3 * c + min(c, FULL)), T * (3 * c + 3 + min(c + 1, FULL))) for c in range(NC)]
NO_EDGE = -1.0e30
TINY = 2.0 ** -60
EP, GT = 128, 3
PT = 2 * GT
GROUP, PAIR = GT * EP, PT * EP
ROWS = (E + 2 * PAIR - 1) // (2 * PAIR)
NPAIR = 2 * ROWS
W = 16
WN = W * NT
SLOTS = W + T + W
LAST = E - (ROWS - 1) * 2 * PAIR
LASTG = E - (E // GROUP) * GROUP
ROUND = 12582912.0
S_PAD = 100000000


class Marks:
    def __init__(self, sem):
        self.sem, self.n = sem, 0

    def inc(self, ins, by=1):
        ins.then_inc(self.sem, by)
        self.n += by
        return self.n


def chain(eng, marks, ins):
    eng.wait_ge(marks.sem, marks.inc(ins))


def pairs_of_blocks(eng, step):
    with eng.Fori(0, NT // 2) as i:
        step(2 * i, 0, i)
        step(2 * i + 1, 1, i)
    step(NT - 1, 0, NT // 2)


class Norm:
    def __init__(self, sem, name, stat, x, h, spare, relu=True):
        self.scales_ready, self.scalar_done = sem(f"{name}_scales"), sem(f"{name}_scalar")
        self.sems = [self.scales_ready, self.scalar_done]
        self.stat, self.x, self.h, self.parts, self.relu = stat, x, h, spare[:, :, 0:6], relu
        self.by_act = NT // 2 if relu else NT * 2 // 5

    def scalar(self, act):
        mean, root, shift = (self.stat[:, k, :] for k in range(3))
        act.wait_ge(self.scales_ready, 1)
        act.activation(root, root, ACT.Sqrt).then_inc(self.scalar_done, 1)
        act.wait_ge(self.scales_ready, 2)
        for t in range(self.by_act):
            last = act.activation(self.h[:, t, :], self.x[:, t, :], ACT.Relu if self.relu else ACT.Identity,
                                  bias=shift[:, t:t + 1], scale=root[:, t:t + 1])
        last.then_inc(self.scalar_done, 1)

    def tile_statistics(self, dve, t):
        return dve.bn_stats(self.parts[:, t, :], self.x[:, t, :])

    def vector(self, dve, m, have_statistics=False):
        mean, var, shift, half = (self.stat[:, k, :] for k in range(4))
        of = lambda k: self.parts[:, :, k]
        if not have_statistics:
            for t in range(NT):
                last = self.tile_statistics(dve, t)
            chain(dve, m, last)
        dve.tensor_tensor(half, of(1), of(4), ALU.subtract)
        dve.tensor_tensor(mean, of(1), of(4), ALU.add)
        chain(dve, m, dve.tensor_tensor(var, of(2), of(5), ALU.add))
        chain(dve, m, dve.tensor_tensor(half, half, half, ALU.mult))
        dve.tensor_scalar(mean, mean, 0.5, None, ALU.mult)
        chain(dve, m, dve.tensor_scalar(var, var, 1.0 / D, 1e-5, ALU.mult, ALU.add))
        dve.scalar_tensor_tensor(out=var, in0=half, scalar=0.25, in1=var, op0=ALU.mult, op1=ALU.add).then_inc(self.scales_ready, 1)
        dve.wait_ge(self.scalar_done, 1)
        chain(dve, m, dve.reciprocal(var, var))
        chain(dve, m, dve.scalar_tensor_tensor(out=shift, in0=mean, scalar=-1.0, in1=var, op0=ALU.mult, op1=ALU.mult))
        dve.sem_inc(self.scales_ready, 1)
        for t in range(self.by_act, NT):
            last = dve.tensor_scalar(self.h[:, t, :], self.x[:, t, :], mean[:, t:t + 1], var[:, t:t + 1], ALU.subtract, ALU.mult)
        chain(dve, m, last)
        if self.relu:
            rest = self.h[:, self.by_act:, :]
            chain(dve, m, dve.tensor_scalar(rest, rest, 0.0, None, ALU.max))
        dve.wait_ge(self.scalar_done, 2)


def prepare(nc, G):
    with ExitStack() as ctx:
        sb = lambda name, shape, dt=FP32: ctx.enter_context(nc.sbuf_tensor(name, shape, dt))
        ps = lambda name, shape, dt=FP32: ctx.enter_context(nc.psum_tensor(name, shape, dt))
        sem = lambda name: ctx.enter_context(nc.semaphore(name))
        d_i = sb("d_i", [ROWS, 2 * PAIR], I32)
        s_i = sb("s_i", [ROWS, 2 * PAIR], I32)
        d_f = sb("d_f", [ROWS, 2 * PAIR])
        s_f = sb("s_f", [ROWS, 2 * PAIR])
        tile_f = sb("tile_f", [ROWS, 2 * PAIR])
        gmm = sb("gmm", [ROWS, 2, 4])
        rows = sb("rows", [NT, 2, 2 * NPAIR])
        pmin = sb("pmin", [NT, NPAIR])
        pmax = sb("pmax", [NT, NPAIR])
        pidx = sb("pidx", [NT, NPAIR])
        bidx = sb("bidx", [NT, 1])
        bnd = sb("bnd", [NT, 2])
        tab = sb("tab", [NT, 3])
        tab_i = sb("tab_i", [NT, 3], I32)
        spn = sb("spn", [NT, 2 * NPAIR])
        work = sb("ln_work", [T, NT, D])
        stat = sb("ln_stat", [T, 4, NT])
        key_ps = ps("key_ps", [EP, 2, 512])
        sp_ps = ps("sp_ps", [EP, 2, 512])
        edges_in = sem("edges_in")
        x_in = sem("x_in")
        s_padded = sem("s_padded")
        consts_ready = sem("consts_ready")
        dve_done = sem("prep_dve_done")
        mm_out = sem("mm_out")
        mm_back = sem("mm_back")
        tab_out = sem("tab_out")
        tab_back = sem("tab_back")
        keys_ready = sem("keys_ready")
        mm_ready = sem("mm_ready")
        tab_ready = sem("tab_ready")
        turned = sem("turned")
        x, h, ident = G["x"], G["h"], G["ident"]
        norm = Norm(sem, "norm0", stat, x, h, work)
        with nc.Block() as block:
            @block.sync
            def _(sp):
                full = (ROWS - 1) * 2 * PAIR
                def rows_of(a, lo, n):
                    return a[lo:lo + n].rearrange("(a n) -> a n", a=1)
                sp.dma_start(d_i[0:ROWS - 1, :], G["dst"][0:full].rearrange("(p n) -> p n", n=2 * PAIR)).then_inc(edges_in, 16)
                sp.dma_start(d_i[ROWS - 1:ROWS, 0:LAST], rows_of(G["dst"], full, LAST)).then_inc(edges_in, 16)
                at = LAST
                while at < 2 * PAIR:
                    n = min(LASTG, 2 * PAIR - at)
                    sp.dma_start(d_i[ROWS - 1:ROWS, at:at + n], rows_of(G["dst"], E - LASTG, n)).then_inc(edges_in, 16)
                    at += n
                sp.wait_ge(s_padded, 1)
                sp.dma_start(s_i[0:ROWS - 1, :], G["src"][0:full].rearrange("(p n) -> p n", n=2 * PAIR)).then_inc(edges_in, 16)
                sp.dma_start(s_i[ROWS - 1:ROWS, 0:LAST], rows_of(G["src"], full, LAST)).then_inc(edges_in, 16)
                sp.dma_start(x[:, :, :], G["x_in"].rearrange("(t p) d -> p t d", p=T)).then_inc(x_in, 16)
                sp.wait_ge(mm_ready, 1)
                sp.dma_start(G["mm_dram"].rearrange("k (p q) -> p k q", q=4), gmm[:, :, :]).then_inc(mm_out, 16)
                sp.wait_ge(mm_out, 16)
                sp.dma_start(rows[:, :, :], G["mm_dram"].unsqueeze(0).broadcast_to([NT, 2, 2 * NPAIR])).then_inc(mm_back, 16)
                sp.dma_start(G["gmin"][0:1, :], G["mm_dram"][0:1, :]).then_inc(mm_back, 16)
                sp.wait_ge(tab_ready, 1)
                sp.dma_start(G["tab_dram"][:, :], tab_i[:, :]).then_inc(tab_out, 16)
                sp.wait_ge(tab_out, 16)
                sp.dma_start(G["ranges"][0:1, :], G["tab_dram"].rearrange("(a b) c -> a (b c)", a=1)).then_inc(tab_back, 16)
                sp.wait_ge(tab_back, 16)

            @block.gpsimd
            def _(pool):
                pool.memset(s_i[:, :], S_PAD).then_inc(s_padded, 1)
                pool.memset(ident[:, :], 0.0).then_inc(consts_ready, 1)
                pool.wait_ge(consts_ready, 1)
                pool.affine_select(out=ident[:, :], in_=ident[:, :], compare_op=ALU.not_equal, fill=1.0,
                                   base=0, pattern=[[-1, 128]], channel_multiplier=1).then_inc(consts_ready, 1)
                pool.iota(G["iota_win"][:, :], [[1, NT], [NT, W]], base=0, channel_multiplier=0,
                          allow_small_or_imprecise_dtypes=True).then_inc(consts_ready, 1)
                pool.iota(G["iota_t"][:, :], [[1, T]], base=0, channel_multiplier=0,
                          allow_small_or_imprecise_dtypes=True).then_inc(consts_ready, 1)
                pool.iota(pidx[:, :], [[1, NPAIR]], base=0, channel_multiplier=0,
                          allow_small_or_imprecise_dtypes=True).then_inc(consts_ready, 1)
                pool.iota(bidx[:, :], [[0, 1]], base=0, channel_multiplier=T,
                          allow_small_or_imprecise_dtypes=True).then_inc(consts_ready, 1)
                pool.memset(G["tiny"][:, :], TINY).then_inc(consts_ready, 1)
                pool.memset(G["agg"][:, :], 0.0).then_inc(consts_ready, 1)

            @block.scalar
            def _(act):
                norm.scalar(act)

            @block.vector
            def _(dve):
                m = Marks(dve_done)
                fills = -(-(2 * PAIR - LAST) // LASTG)
                dve.wait_ge(edges_in, 16 * (4 + fills))
                q4 = lambda t: t[:, :].rearrange("p (q n) -> p q n", q=4)
                chain(dve, m, dve.tensor_copy(d_f[:, :], d_i[:, :]))
                chain(dve, m, dve.tensor_reduce(gmm[:, 0, :], q4(d_f), AX.X, ALU.min))
                dve.tensor_reduce(gmm[:, 1, :], q4(d_f), AX.X, ALU.max).then_inc(mm_ready, 1)
                chain(dve, m, dve.tensor_copy(s_f[:, :], s_i[:, :]))
                chain(dve, m, dve.tensor_scalar(tile_f[:, :], s_f[:, :], 1.0 / T, 0.5 / T - 0.5, ALU.mult, ALU.add))
                chain(dve, m, dve.tensor_scalar(tile_f[:, :], tile_f[:, :], ROUND, None, ALU.add))
                chain(dve, m, dve.tensor_scalar(tile_f[:, :], tile_f[:, :], ROUND, None, ALU.subtract))
                chain(dve, m, dve.scalar_tensor_tensor(out=s_f[:, :], in0=tile_f[:, :], scalar=-float(T), in1=s_f[:, :],
                                                       op0=ALU.mult, op1=ALU.add))
                chain(dve, m, dve.tensor_tensor(q4(d_f), q4(d_f), gmm[:, 0, :].unsqueeze(2).broadcast_to([ROWS, 4, GROUP]),
                                                ALU.subtract))
                dve.scalar_tensor_tensor(out=d_f[:, :], in0=d_f[:, :], scalar=float(NT), in1=tile_f[:, :],
                                         op0=ALU.mult, op1=ALU.add).then_inc(keys_ready, 1)
                for j in range(2):
                    for k, (bank, out) in enumerate(((key_ps, G["key"]), (sp_ps, G["place"]))):
                        dve.wait_ge(turned, 2 * j + k + 1)
                        dve.tensor_copy(out[:, :].rearrange("e (p j i) -> e j i p", j=2, i=PT)[:, j],
                                        bank[:, j, 0:PT * ROWS].rearrange("e (i p) -> e i p", i=PT))
                dve.wait_ge(consts_ready, 8)
                dve.wait_ge(mm_back, 32)
                both = rows[:, :, :].rearrange("b k (p g) -> b k p g", g=2)
                chain(dve, m, dve.tensor_reduce(pmin[:, :], both[:, 0], AX.X, ALU.min))
                chain(dve, m, dve.tensor_reduce(pmax[:, :], both[:, 1], AX.X, ALU.max))
                chain(dve, m, dve.tensor_scalar(bnd[:, 0:1], bidx[:, :], float(T - 1), None, ALU.add))
                chain(dve, m, dve.tensor_scalar(pmax[:, :], pmax[:, :], bidx[:, 0:1], 1000.0, ALU.is_lt, ALU.mult))
                chain(dve, m, dve.tensor_tensor(pmax[:, :], pmax[:, :], pidx[:, :], ALU.add))
                chain(dve, m, dve.tensor_reduce(tab[:, 0:1], pmax[:, :], AX.X, ALU.min))
                chain(dve, m, dve.tensor_scalar(pmin[:, :], pmin[:, :], bnd[:, 0:1], None, ALU.is_le))
                chain(dve, m, dve.tensor_scalar(pidx[:, :], pidx[:, :], 1.0, None, ALU.add))
                chain(dve, m, dve.tensor_tensor(pmin[:, :], pmin[:, :], pidx[:, :], ALU.mult))
                chain(dve, m, dve.tensor_reduce(tab[:, 1:2], pmin[:, :], AX.X, ALU.max))
                chain(dve, m, dve.tensor_scalar(tab[:, 0:1], tab[:, 0:1], float(NPAIR - 2), None, ALU.min))
                chain(dve, m, dve.tensor_scalar(bnd[:, 1:2], tab[:, 0:1], 2.0, None, ALU.add))
                chain(dve, m, dve.tensor_tensor(tab[:, 1:2], tab[:, 1:2], bnd[:, 1:2], ALU.max))
                chain(dve, m, dve.tensor_tensor(spn[:, :], rows[:, 1, :], rows[:, 0, :], ALU.subtract))
                chain(dve, m, dve.tensor_reduce(tab[:, 2:3], spn[:, :], AX.X, ALU.max))
                chain(dve, m, dve.tensor_scalar(tab[:, 2:3], tab[:, 2:3], 1.0 / W, 0.5 / W - 0.5, ALU.mult, ALU.add))
                chain(dve, m, dve.tensor_scalar(tab[:, 2:3], tab[:, 2:3], ROUND, None, ALU.add))
                chain(dve, m, dve.tensor_scalar(tab[:, 2:3], tab[:, 2:3], ROUND - 1.0, None, ALU.subtract))
                dve.tensor_copy(tab_i[:, :], tab[:, :]).then_inc(tab_ready, 1)
                dve.tensor_scalar(G["gmin"][0:1, :], G["gmin"][0:1, :], float(W), None, ALU.add)
                dve.wait_ge(x_in, 16)
                norm.vector(dve, m)

            @block.tensor
            def _(pe):
                pe.wait_ge(consts_ready, 2)
                pe.wait_ge(keys_ready, 1)
                for j in range(2):
                    for bank, src in ((key_ps, d_f), (sp_ps, s_f)):
                        for i in range(PT):
                            at = j * PAIR + i * EP
                            last = pe.transpose(bank[:, j, i * ROWS:(i + 1) * ROWS], src[:, at:at + EP],
                                                ident[0:ROWS, 0:ROWS])
                        last.then_inc(turned, 1)


def build_counts(nc, G):
    BANKS = 3
    last_in_bank = [c - BANKS if c >= BANKS else max(k for k in range(NC) if k % BANKS == c) - NC for c in range(NC)]
    with ExitStack() as ctx:
        sb = lambda name, shape, dt=FP32: ctx.enter_context(nc.sbuf_tensor(name, shape, dt))
        ps = lambda name, shape, dt=FP32: ctx.enter_context(nc.psum_tensor(name, shape, dt))
        sem = lambda name: ctx.enter_context(nc.semaphore(name))
        blk = [sb(f"blk{p}", [T, NT, SLOTS]) for p in range(2)]
        lnrow = [sb(f"lnrow{p}", [T, N]) for p in range(2)]
        crow = sb("crow", [T, N])
        hot_key = sb("hot_key", [EP, PT, WN], BF16)
        hot_place = sb("hot_place", [EP, PT, T], BF16)
        staged = sb("staged", [T, 2, WN])
        posf = sb("posf", [1, 2 * NPAIR])
        posi = sb("posi", [1, 2 * NPAIR], I32)
        shift = sb("shift", [EP, 1])
        dtile = sb("dtile", [T, T])
        deg_parts = [sb(f"deg_parts{p}", [T, NC]) for p in range(2)]
        h_tile = [sb(f"h_tile{p}", [T, D]) for p in range(2)]
        win = [ps(f"win{k}", [T, WN]) for k in range(2)]
        turn = [ps(f"turn{k}", [T, C4]) for k in range(BANKS)]
        acc = [ps(f"acc{k}", [D, C4]) for k in range(BANKS)]
        ranges, h, sums, ident, passed = G["ranges"], G["h"], G["agg"], G["ident"], G["passed"]
        hot_ready = sem("hot_ready")
        group_done = sem("group_done")
        win_copied = sem("win_copied")
        added = sem("added")
        pos_made = sem("pos_made")
        shift_made = sem("shift_made")
        zeroed = sem("zeroed")
        blk_full = sem("blk_full")
        blk_used = sem("blk_used")
        counts_out = [sem(f"counts_out{p}") for p in range(2)]
        turn_ready = sem("turn_ready")
        crow_made = sem("crow_made")
        bank_read = sem("bank_read")
        bias_made = sem("bias_made")
        bias_out = [sem(f"bias_out{p}") for p in range(2)]
        part_filled = sem("part_filled")
        part_added = sem("part_added")
        h_staged = sem("h_staged")
        deg_done = sem("deg_done")
        diag_ready = sem("diag_ready")
        diag_read = sem("diag_read")

        def start(eng):
            turns = eng.alloc_register("turns")
            eng.reg_mov(turns, 0)
            rounds = eng.value_load(ranges[0:1, 2:3], min_val=1, max_val=(N + W - 1) // W + 1)
            return turns, rounds

        def over_pairs(eng, b, turns, rounds, body, each_round=None, after_round=None):
            lo = eng.value_load(ranges[0:1, bass.ds(3 * b, 1)], min_val=0, max_val=NPAIR - 2)
            hi = eng.value_load(ranges[0:1, bass.ds(3 * b + 1, 1)], min_val=2, max_val=NPAIR)
            with eng.Fori(0, rounds) as _:
                if each_round:
                    each_round()
                with eng.Fori(lo, hi) as pair:
                    it = eng.snap(turns, min_val=0, max_val=2 ** 24)
                    body(pair, it)
                    eng.reg_add(turns, turns, 1)
                if after_round:
                    after_round()

        with nc.Block() as block:
            @block.sync
            def _(sp):
                for p in range(2):
                    sp.sem_inc(counts_out[p], 16)
                    sp.sem_inc(bias_out[p], 16)

                def step(b, p, i2):
                    sp.wait_ge(blk_full, b + 1)
                    sp.dma_start(G["counts_dram"][:, :, bass.ds(b * T, T)].rearrange("t s d -> s t d"), blk[p][:, :, W:W + T]).then_inc(counts_out[p], 16)
                    sp.wait_ge(bias_made, b * NC + 2 * NC)
                    sp.dma_start(G["bias_dram"][b, :, :], lnrow[p][:, :]).then_inc(bias_out[p], 16)
                pairs_of_blocks(sp, step)
                for p in range(2):
                    blocks = (NT + 1 - p) // 2
                    sp.wait_ge(counts_out[p], 16 * (blocks + 1))
                    sp.wait_ge(bias_out[p], 16 * (blocks + 1))

            @block.vector
            def _(dve):
                turns, rounds = start(dve)
                past = dve.alloc_register("rounds_past")
                dve.reg_mov(past, 0)
                dve.sem_inc(part_added, NC)
                dve.sem_inc(bias_made, NC)
                dve.sem_inc(shift_made, 1)
                dve.sem_inc(deg_done, 2)
                dve.sem_inc(diag_read, 1)

                lo, first, hi = (dve.alloc_register(f"pair_{k}") for k in ("lo", "first", "hi"))
                pair_no = lambda r, most: dve.snap(r, min_val=0, max_val=most)

                def made(b):
                    dve.wait_ge(shift_made, dve.snap(past, min_val=0, max_val=2 ** 24) + (b + 1))
                    dve.sem_inc(passed, 1)

                def body(pair, it):
                    for k in range(2):
                        dve.wait_ge(group_done, 2 * it + (k + 1))
                        for i in range(GT * k, GT * k + GT):
                            at = bass.ds(pair * PT + i, 1)
                            dve.tensor_scalar(hot_key[:, i, :], G["iota_win"][:, :], G["key"][:, at], shift[:, 0:1],
                                              ALU.subtract, ALU.is_equal)
                            last = dve.tensor_scalar(hot_place[:, i, :], G["iota_t"][:, :], G["place"][:, at], None,
                                                     ALU.is_equal)
                        last.then_inc(hot_ready, 1)
                    dve.reg_add(turns, turns, 1)

                def first_pair(b):
                    dve.reg_load(lo, ranges[0:1, bass.ds(3 * b, 1)])
                    dve.reg_load(hi, ranges[0:1, bass.ds(3 * b + 1, 1)])
                    made(b)
                    dve.memset(shift[:, :], 0.0).then_inc(shift_made, 1)
                    made(b + 1)
                    body(pair_no(lo, NPAIR - 2), dve.snap(turns, min_val=0, max_val=2 ** 24))
                    dve.reg_add(first, lo, 1)
                first_pair(0)

                def step(b, p, i2, final=False):
                    with dve.Fori(0, rounds) as _:
                        with dve.Fori(pair_no(first, NPAIR - 1), pair_no(hi, NPAIR)) as pair:
                            body(pair, dve.snap(turns, min_val=0, max_val=2 ** 24))
                        dve.wait_ge(hot_ready, 2 * dve.snap(turns, min_val=0, max_val=2 ** 24))
                        dve.tensor_scalar(shift[:, :], shift[:, :], float(WN), None, ALU.subtract).then_inc(shift_made, 1)
                        dve.reg_add(past, past, 1)
                        dve.reg_mov(first, lo)
                        made(b + 1)
                    if not final:
                        first_pair(b + 1)
                    for c, (a, z) in enumerate(CHUNKS):
                        dve.wait_ge(bank_read, b * NC + (c + 1 + NC))
                        here = lnrow[p][:, a:z]
                        dve.scalar_tensor_tensor(out=here, in0=here, scalar=-NO_EDGE, in1=here, op0=ALU.mult, op1=ALU.min
                                                 ).then_inc(bias_made, 1)
                        dve.wait_ge(part_filled, b * NC + (c + 1 + NC))
                        dve.wait_ge(part_added, b * NC + (c + 1))
                        dve.tensor_tensor(sums[:, a:z], sums[:, a:z], acc[c % BANKS][:, 0:z - a], ALU.add).then_inc(part_added, 1)
                    dve.tensor_reduce(G["deg"][:, bass.ds(b, 1)], deg_parts[p][:, :], AX.X, ALU.add).then_inc(deg_done, 1)
                    dve.wait_ge(diag_ready, b + 1)
                    dve.tensor_reduce(G["selfc"][:, bass.ds(b, 1)], dtile[:, :], AX.X, ALU.add).then_inc(diag_read, 1)
                with dve.Fori(0, NT // 2) as i:
                    step(2 * i, 0, i)
                    step(2 * i + 1, 1, i)
                step(NT - 1, 0, NT // 2, final=True)

            @block.tensor
            def _(pe):
                turns, rounds = start(pe)
                pe.sem_inc(group_done, 2)
                pe.sem_inc(blk_used, 1)
                pe.sem_inc(part_filled, NC)

                def step(b, p, i2):
                    def body(pair, it):
                        for k in range(2):
                            pe.wait_ge(win_copied, 2 * it + (k + 1))
                            pe.wait_ge(hot_ready, 2 * it + (k + 1))
                            for i in range(GT * k, GT * k + GT):
                                last = pe.matmul(win[k][:, :], hot_place[:, i, :], hot_key[:, i, :],
                                                 start=(i == GT * k), stop=(i == GT * k + GT - 1))
                            last.then_inc(group_done, 1)
                    over_pairs(pe, b, turns, rounds, body)
                    pe.wait_ge(h_staged, b + 1)
                    pe.wait_ge(blk_full, b + 1)

                    def turn_chunk(c):
                        a, z = CHUNKS[c]
                        pe.wait_ge(bank_read, b * NC + (last_in_bank[c] + 1 + NC))
                        for j in range((z - a) // T):
                            last = pe.transpose(turn[c % BANKS][:, j * T:(j + 1) * T], blk[p][:, a // T + j, W:W + T], ident[0:T, 0:T])
                        last.then_inc(turn_ready, 1)

                    def sum_chunk(c):
                        a, z = CHUNKS[c]
                        pe.wait_ge(crow_made, b * NC + (c + 1))
                        pe.wait_ge(part_added, b * NC + (last_in_bank[c] + 1 + NC))
                        pe.matmul(acc[c % BANKS][:, 0:z - a], h_tile[p][:, :], crow[:, a:z],
                                  start=True, stop=True).then_inc(part_filled, 1)
                    turn_chunk(0)
                    for c in range(1, NC):
                        turn_chunk(c)
                        if c > 1:
                            sum_chunk(c - 2)
                    pe.wait_ge(turn_ready, b * NC + NC)
                    pe.sem_inc(blk_used, 1)
                    sum_chunk(NC - 2)
                    sum_chunk(NC - 1)
                pairs_of_blocks(pe, step)

            @block.scalar
            def _(act):
                turns, rounds = start(act)
                act.sem_inc(win_copied, 2)
                act.sem_inc(bank_read, NC)
                act.preload_act_table(ACT.Ln)

                def step(b, p, i2):
                    def body(pair, it):
                        for k in range(2):
                            act.wait_ge(added, 2 * it + (k + 1))
                            act.wait_ge(group_done, 2 * it + (k + 3))
                            act.activation(staged[:, k, :], win[k][:, :], ACT.Copy).then_inc(win_copied, 1)
                    over_pairs(act, b, turns, rounds, body)
                    act.wait_ge(bias_out[p], 16 * i2 + 16)
                    act.wait_ge(deg_done, b + 1)
                    for c, (a, z) in enumerate(CHUNKS):
                        turned = turn[c % BANKS][:, 0:z - a]
                        act.wait_ge(turn_ready, b * NC + (c + 1))
                        act.wait_ge(part_filled, b * NC + (c + 1))
                        act.activation(crow[:, a:z], turned, ACT.Copy, accum_out=deg_parts[p][:, c:c + 1]).then_inc(crow_made, 1)
                        act.activation(lnrow[p][:, a:z], turned, ACT.Ln, bias=G["tiny"][0:T, :], scale=2.0).then_inc(bank_read, 1)
                pairs_of_blocks(act, step)

            @block.gpsimd
            def _(pool):
                turns, rounds = start(pool)
                past = pool.alloc_register("rounds_past")
                pool.reg_mov(past, 0)
                pool.sem_inc(added, 2)
                base = G["gmin"]

                def clear(p):
                    pool.memset(blk[p][:, :, :], 0.0).then_inc(zeroed, 1)
                clear(0)

                def stage(b, p):
                    pool.tensor_copy(h_tile[p][:, :].unsqueeze(1), h[:, bass.ds(b, 1), :]).then_inc(h_staged, 1)
                stage(0, 0)
                pool.tensor_copy(posf[:, :], base[0:1, :]).then_inc(pos_made, 1)

                def step(b, p, i2, last=False):
                    def made(k):
                        pool.wait_ge(pos_made, 2 * pool.snap(past, min_val=0, max_val=2 ** 24) + (2 * b + k))
                        pool.sem_inc(passed, 1)

                    def each_round():
                        made(1)
                        pool.tensor_scalar(posi[:, :], posf[:, :], 0.0, float(W + T), ALU.max, ALU.min).then_inc(pos_made, 1)
                        pool.tensor_scalar(posf[:, :], posf[:, :], float(W), None, ALU.add).then_inc(pos_made, 1)
                        made(3)
                        pool.wait_ge(zeroed, b + 1)
                        pool.sem_inc(passed, 1)

                    def body(pair, it):
                        pos = [pool.value_load(posi[0:1, bass.ds(pair * 2 + k, 1)], min_val=0, max_val=W + T)
                               for k in range(2)]
                        for k in range(2):
                            pool.wait_ge(win_copied, 2 * it + (k + 3))
                            pool.wait_ge(added, 2 * it + (k + 2))
                            here = blk[p][:, :, bass.ds(pos[k], W)]
                            pool.tensor_tensor(here, here, staged[:, k, :].rearrange("s (t w) -> s t w", w=W), ALU.add).then_inc(added, 1)

                    def after_round():
                        pool.reg_add(past, past, 1)
                    over_pairs(pool, b, turns, rounds, body, each_round, after_round)
                    it = pool.snap(turns, min_val=0, max_val=2 ** 24)
                    pool.wait_ge(added, 2 * it + 2)
                    pool.sem_inc(blk_full, 1)
                    on = blk[p][:, bass.ds(b, 1), W:W + T]
                    pool.wait_ge(diag_read, b + 1)
                    pool.tensor_tensor(dtile[:, :].unsqueeze(1), on, ident[0:T, 0:T].unsqueeze(1), ALU.mult).then_inc(diag_ready, 1)
                    if last:
                        return
                    pool.tensor_scalar(base[0:1, :], base[0:1, :], float(T), None, ALU.subtract).then_inc(pos_made, 1)
                    made(2)
                    pool.tensor_copy(posf[:, :], base[0:1, :]).then_inc(pos_made, 1)
                    pool.wait_ge(part_filled, b * NC + NC)
                    pool.sem_inc(passed, 1)
                    stage(b + 1, 1 - p)
                    if p == 0:
                        pool.wait_ge(counts_out[1], 16 * i2 + 16)
                    else:
                        pool.wait_ge(counts_out[0], 16 * i2 + 32)
                    pool.wait_ge(blk_used, b + 1)
                    pool.sem_inc(passed, 1)
                    clear(1 - p)
                with pool.Fori(0, NT // 2) as i:
                    step(2 * i, 0, i)
                    step(2 * i + 1, 1, i)
                step(NT - 1, 0, NT // 2, last=True)


class Banks:
    def __init__(self, tiles, filled, read, stages):
        self.tiles, self.filled, self.read = tiles, filled, read
        self.readers, self.first = [], {}
        for name, n, reader in stages:
            self.first[name] = len(self.readers)
            self.readers += [reader] * n

    def fill(self, pe, name, i):
        q = self.first[name] + i
        before = q - len(self.tiles)
        if before >= 0:
            who = self.readers[before]
            pe.wait_ge(self.read[who], self.readers[:before + 1].count(who))
        return self.tiles[q % len(self.tiles)]

    def full(self, eng, name, i):
        q = self.first[name] + i
        eng.wait_ge(self.filled, q + 1)
        return self.tiles[q % len(self.tiles)]

    def done(self, eng, name, n=None):
        at = self.first[name]
        who = self.readers[at]
        n = n or next((k for k in range(at, len(self.readers) + 1)
                       if k in self.first.values() and k > at or k == len(self.readers))) - at
        eng.wait_ge(self.read[who], self.readers[:at + n].count(who))


def bank_set(nc, ctx, name, stages, count=4):
    tiles = [ctx.enter_context(nc.psum_tensor(f"{name}_bank{k}", [128, 512], FP32)) for k in range(count)]
    filled = ctx.enter_context(nc.semaphore(f"{name}_filled"))
    read = {who: ctx.enter_context(nc.semaphore(f"{name}_read_{who}")) for who in ("act", "dve")}
    return Banks(tiles, filled, read, stages)


def tiles_of(c):
    a, z = CHUNKS[c]
    return range(a // T, z // T)


def pe_turn(pe, banks, name, src, width, ident):
    for c in range(NC):
        bank = banks.fill(pe, name, c)
        for j, t in enumerate(tiles_of(c)):
            last = pe.transpose(bank[0:width, j * T:(j + 1) * T], src[:, t, 0:width], ident[0:T, 0:T])
        last.then_inc(banks.filled, 1)


def pe_columns(pe, banks, name, weight, src):
    for c, (a, z) in enumerate(CHUNKS):
        bank = banks.fill(pe, name, c)
        pe.matmul(bank[0:weight.shape[1], 0:z - a], weight, src[:, a:z], start=True, stop=True).then_inc(banks.filled, 1)


def pe_rows(pe, banks, name, cols, weights):
    width = weights[0].shape[1]
    for c in range(NC):
        bank = banks.fill(pe, name, c)
        for j, t in enumerate(tiles_of(c)):
            for k, (col, w) in enumerate(zip(cols, weights)):
                last = pe.matmul(bank[0:T, j * width:(j + 1) * width], col[:, t * T:(t + 1) * T], w,
                                 start=(k == 0), stop=(k == len(cols) - 1))
        last.then_inc(banks.filled, 1)


def act_columns(act, banks, name, out, rows=128, func=None, bias=None, scale=1.0):
    for c, (a, z) in enumerate(CHUNKS):
        bank = banks.full(act, name, c)
        if bias is None:
            last = act.activation(out[:, a:z], bank[0:rows, 0:z - a], func or ACT.Copy, scale=scale)
        else:
            last = act.activation(out[:, a:z], bank[0:rows, 0:z - a], func or ACT.Identity, bias=bias, scale=scale)
        last.then_inc(banks.read["act"], 1)


def rows_view(bank, c, width):
    n = len(tiles_of(c))
    return bank[0:T, 0:n * width].rearrange("p (t d) -> p t d", d=width)


def layers_0_1(nc, G):
    HID = 16
    with ExitStack() as ctx:
        sb = lambda name, shape, dt=FP32: ctx.enter_context(nc.sbuf_tensor(name, shape, dt))
        ps = lambda name, shape, dt=FP32: ctx.enter_context(nc.psum_tensor(name, shape, dt))
        sem = lambda name: ctx.enter_context(nc.semaphore(name))
        x, h, agg, ident = G["x"], G["h"], G["agg"], G["ident"]
        cols = sb("cols0", [128, N])
        hid = [sb(f"hid{j}", [128, N]) for j in range(2)]
        work = sb("work0", [T, NT, D])
        stat = sb("stat0", [T, 4, NT])
        small = sb("small0", [T, 3, NT])
        w1 = sb("w1_0", [D, 2 * D])
        w2 = sb("w2_0", [128, 2, D])
        b1 = sb("b1_0", [128, 2])
        b2 = sb("b2_0", [T, D])
        cw1 = sb("cw1", [D, HID])
        cb1 = sb("cb1", [T, HID])
        cw2 = sb("cw2", [HID, D])
        cb2 = sb("cb2", [T, D])
        u = sb("u", [T, NT, HID])
        conv = sb("conv", [T, NT, HID])
        vcols = sb("vcols", [HID, N])
        counts = [sb(f"counts{p}", [T, N]) for p in range(2)]
        u_tile = [sb(f"u_tile{p}", [T, HID]) for p in range(2)]
        weights_in = sem("weights_in0")
        agg_ready = sem("l0_sum_ready")
        h_ready = sem("l1_h_ready")
        norms = [Norm(sem, f"norm{k + 1}", stat, x, h, work) for k in range(2)]
        deg_ready = sem("deg_ready")
        deg_root = sem("deg_root")
        u_staged = sem("u_staged")
        tile_used = sem("tile_used")
        counts_in = [sem(f"counts_in{p}") for p in range(2)]
        sum_copied = sem("sum_copied")
        rows_turned = sem("rows_turned")
        u_ready = sem("u_ready")
        soft_in = sem("soft_in")
        soft_out = sem("soft_out")
        each = lambda v, n: v.unsqueeze(2).broadcast_to([T, NT, n])
        every = lambda v, n: v.unsqueeze(1).broadcast_to([T, NT, n])

        with ExitStack() as mlp:
            banks = bank_set(nc, mlp, "l0", [
                ("agg", NC, "dve"), ("hid0", NC, "act"), ("hid1", NC, "act"), ("mlp", NC, "dve"),
                ("h1", NC, "act"), ("u", 1, "dve")])
            dve_done = sem("l0_dve_done")
            with nc.Block() as block:
                @block.sync
                def _(sp):
                    for dst, src in (
                            (w1[:, :], G["L0_gnn_W1"]), (w2[:, :, :], G["L0_gnn_W2"].rearrange("(j k) d -> k j d", j=2)),
                            (b1[:, :], G["L0_gnn_b1"].rearrange("(j k) -> k j", j=2)),
                            (b2[:, :], G["L0_gnn_b2"].unsqueeze(0).broadcast_to([T, D])),
                            (cw1[:, :], G["L1_gnn_W1"]), (cw2[:, :], G["L1_gnn_W2"]),
                            (cb1[:, :], G["L1_gnn_b1"].unsqueeze(0).broadcast_to([T, HID])),
                            (cb2[:, :], G["L1_gnn_b2"].unsqueeze(0).broadcast_to([T, D]))):
                        with nc.allow_non_contiguous_dma(reason="small weights"):
                            sp.dma_start(dst, src).then_inc(weights_in, 16)

                @block.tensor
                def _(pe):
                    pe.wait_ge(weights_in, 16 * 8)
                    pe.wait_ge(agg_ready, 1)
                    pe_turn(pe, banks, "agg", work, D, ident)
                    banks.done(pe, "agg")
                    for j in range(2):
                        pe_columns(pe, banks, f"hid{j}", w1[:, j * D:(j + 1) * D], cols)
                    banks.done(pe, "hid1")
                    pe_rows(pe, banks, "mlp", hid, [w2[:, j, :] for j in range(2)])
                    pe.wait_ge(h_ready, 1)
                    pe_turn(pe, banks, "h1", h, D, ident)
                    banks.done(pe, "h1")
                    bank = banks.fill(pe, "u", 0)
                    for t in range(NT):
                        last = pe.matmul(bank[0:T, t * HID:(t + 1) * HID], cols[:, t * T:(t + 1) * T], cw1[:, :],
                                         start=True, stop=True)
                    last.then_inc(banks.filled, 1)

                @block.scalar
                def _(act):
                    act.wait_ge(deg_ready, 1)
                    act.activation(G["dinv"][:, :], G["dinv"][:, :], ACT.Sqrt).then_inc(deg_root, 1)
                    act.wait_ge(weights_in, 16 * 8)
                    for j in range(2):
                        act_columns(act, banks, f"hid{j}", hid[j], func=ACT.Relu, bias=b1[:, j:j + 1])
                    norms[0].scalar(act)
                    act_columns(act, banks, "h1", cols)

                @block.vector
                def _(dve):
                    m = Marks(dve_done)
                    deg, coef = G["deg"][:, :], small[:, 0, :]
                    chain(dve, m, dve.tensor_scalar(G["has_in"][:, :], deg, 0.0, None, ALU.is_gt))
                    dve.tensor_scalar(G["dinv"][:, :], deg, 1.0, None, ALU.add).then_inc(deg_ready, 1)
                    chain(dve, m, dve.tensor_scalar(coef, G["selfc"][:, :], -1.0, 1.0, ALU.mult, ALU.add))
                    dve.tensor_tensor(work[:, :, :], h[:, :, :], each(coef, D), ALU.mult).then_inc(agg_ready, 1)
                    for c, (a, z) in enumerate(CHUNKS):
                        bank = banks.full(dve, "agg", c)
                        dve.tensor_tensor(cols[:, a:z], agg[:, a:z], bank[:, 0:z - a], ALU.add).then_inc(banks.read["dve"], 1)
                    dve.wait_ge(deg_root, 1)
                    chain(dve, m, dve.reciprocal(G["dinv"][:, :], G["dinv"][:, :]))
                    dve.wait_ge(weights_in, 16 * 8)
                    chain(dve, m, dve.tensor_tensor(x[:, :, :], x[:, :, :], every(b2[:, :], D), ALU.add))
                    for c in range(NC):
                        ts = tiles_of(c)
                        bank = banks.full(dve, "mlp", c)
                        here = x[:, ts[0]:ts[-1] + 1, :]
                        dve.tensor_tensor(here, here, rows_view(bank, c, D), ALU.add).then_inc(banks.read["dve"], 1)
                    banks.done(dve, "mlp")
                    norms[0].vector(dve, m)
                    dve.sem_inc(h_ready, 1)
                    bank = banks.full(dve, "u", 0)
                    dve.tensor_tensor(u[:, :, :], bank[0:T, 0:NT * HID].rearrange("p (t d) -> p t d", d=HID),
                                      each(G["dinv"][:, :], HID), ALU.mult).then_inc(banks.read["dve"], 1)

        with ExitStack() as convs:
            sum_ps = [convs.enter_context(nc.psum_tensor(f"conv_sum{c}", [HID, C4], FP32)) for c in range(NC)]
            rows_ps = convs.enter_context(nc.psum_tensor("conv_rows", [T, NT * HID], FP32))
            dve_done = sem("conv_dve_done")
            with nc.Block() as block:
                @block.sync
                def _(sp):
                    def load(t, p):
                        sp.dma_start(counts[p][:, :], G["counts_dram"][t, :, :]).then_inc(counts_in[p], 16)
                    for r in range(2):
                        if r:
                            sp.wait_ge(tile_used, NT * r)
                        load(0, 0)
                        load(1, 1)
                        with sp.Fori(0, NT // 2 - 1) as i:
                            for p in range(2):
                                sp.wait_ge(tile_used, NT * r + 2 * i + (p + 1))
                                load(2 * i + (p + 2), p)
                        sp.wait_ge(tile_used, NT * r + NT - 2)
                        load(NT - 1, 0)

                @block.gpsimd
                def _(pool):
                    for r in range(2):
                        if r:
                            pool.wait_ge(u_ready, r)

                        def stage(t, p, guard=True):
                            if guard:
                                pool.wait_ge(tile_used, NT * r + t - 1)
                                pool.sem_inc(G["passed"], 1)
                            pool.tensor_copy(u_tile[p][:, :].unsqueeze(1), u[:, bass.ds(t, 1), :]).then_inc(u_staged, 1)
                        stage(0, 0, guard=False)
                        stage(1, 1, guard=False)
                        with pool.Fori(1, NT // 2) as i:
                            stage(2 * i, 0)
                            stage(2 * i + 1, 1)
                        stage(NT - 1, 0)

                @block.tensor
                def _(pe):
                    for r in range(2):
                        def tile(t, p, half, first=False, last=False):
                            pe.wait_ge(counts_in[p], 16 * half + 16 * ((NT + 1 - p) // 2 * r + 1))
                            pe.wait_ge(u_staged, NT * r + t + 1)
                            for c, (a, z) in enumerate(CHUNKS):
                                done = pe.matmul(sum_ps[c][:, 0:z - a], u_tile[p][:, :], counts[p][:, a:z], start=first, stop=last)
                            done.then_inc(tile_used, 1)
                        tile(0, 0, 0, first=True)
                        with pe.Fori(0, NT // 2 - 1) as i:
                            tile(2 * i + 1, 1, i)
                            tile(2 * i + 2, 0, i + 1)
                        tile(NT - 2, 1, NT // 2 - 1)
                        tile(NT - 1, 0, NT // 2, last=True)
                        pe.wait_ge(sum_copied, NC * (r + 1))
                        for t in range(NT):
                            last = pe.transpose(rows_ps[:, t * HID:(t + 1) * HID], vcols[:, t * T:(t + 1) * T], ident[0:HID, 0:HID])
                        last.then_inc(rows_turned, 1)

                @block.scalar
                def _(act):
                    for r in range(2):
                        act.wait_ge(tile_used, NT * (r + 1))
                        if r:
                            act.wait_ge(rows_turned, r)
                        for c, (a, z) in enumerate(CHUNKS):
                            act.activation(vcols[:, a:z], sum_ps[c][:, 0:z - a], ACT.Copy).then_inc(sum_copied, 1)

                @block.vector
                def _(dve):
                    m = Marks(dve_done)
                    turned = rows_ps[:, :].rearrange("p (t d) -> p t d", d=HID)
                    dve.wait_ge(rows_turned, 1)
                    chain(dve, m, dve.tensor_tensor(conv[:, :, :], turned, u[:, :, :], ALU.add))
                    chain(dve, m, dve.tensor_tensor(conv[:, :, :], conv[:, :, :], each(G["dinv"][:, :], HID), ALU.mult))
                    chain(dve, m, dve.tensor_tensor(conv[:, :, :], conv[:, :, :], every(cb1[:, :], HID), ALU.add))
                    chain(dve, m, dve.tensor_scalar(conv[:, :, :], conv[:, :, :], 0.0, None, ALU.max))
                    dve.wait_ge(u_staged, NT)
                    dve.tensor_tensor(u[:, :, :], conv[:, :, :], each(G["dinv"][:, :], HID), ALU.mult).then_inc(u_ready, 1)
                    dve.wait_ge(u_ready, 1)
                    dve.wait_ge(rows_turned, 2)
                    chain(dve, m, dve.tensor_tensor(conv[:, :, :], turned, u[:, :, :], ALU.add))
                    chain(dve, m, dve.tensor_tensor(conv[:, :, :], conv[:, :, :], each(G["dinv"][:, :], HID), ALU.mult))

        with ExitStack() as soft:
            banks = bank_set(nc, soft, "l1", [("v", NC, "act"), ("y", NC, "dve")])
            dve_done = sem("l1_dve_done")
            with nc.Block() as block:
                @block.tensor
                def _(pe):
                    pe_turn(pe, banks, "v", conv, HID, ident)
                    banks.done(pe, "v")
                    pe_rows(pe, banks, "y", [vcols], [cw2[:, :]])

                @block.scalar
                def _(act):
                    act_columns(act, banks, "v", vcols, rows=HID)
                    act.wait_ge(soft_in, 1)
                    act.activation(work[:, :, :], work[:, :, :], ACT.Exp).then_inc(soft_out, 1)
                    act.wait_ge(soft_in, 2)
                    act.activation(small[:, 1, :], small[:, 1, :], ACT.Ln).then_inc(soft_out, 1)
                    norms[1].scalar(act)

                @block.vector
                def _(dve):
                    m = Marks(dve_done)
                    y = agg[0:T, 0:NT * D].rearrange("p (t d) -> p t d", d=D)
                    for c in range(NC):
                        ts = tiles_of(c)
                        bank = banks.full(dve, "y", c)
                        dve.tensor_tensor(y[:, ts[0]:ts[-1] + 1, :], rows_view(bank, c, D),
                                          cb2[:, :].unsqueeze(1).broadcast_to([T, len(ts), D]), ALU.add).then_inc(banks.read["dve"], 1)
                    banks.done(dve, "y")
                    big, total = small[:, 0, :], small[:, 1, :]
                    chain(dve, m, dve.tensor_reduce(big, y, AX.X, ALU.max))
                    chain(dve, m, dve.tensor_tensor(y, y, each(big, D), ALU.subtract))
                    dve.tensor_copy(work[:, :, :], y).then_inc(soft_in, 1)
                    dve.wait_ge(soft_out, 1)
                    dve.tensor_reduce(total, work[:, :, :], AX.X, ALU.add).then_inc(soft_in, 1)
                    chain(dve, m, dve.tensor_tensor(x[:, :, :], x[:, :, :], y, ALU.add))
                    dve.wait_ge(soft_out, 2)
                    chain(dve, m, dve.tensor_tensor(x[:, :, :], x[:, :, :], each(total, D), ALU.subtract))
                    norms[1].vector(dve, m)


ACT_COPIES = {"attention": (1, 3, 5)}


class Turned:
    def __init__(self, nbanks, ready, copied, by_act):
        self.nbanks, self.ready, self.copied = nbanks, ready, copied
        self.who = ["act" if c in by_act else "dve" for c in range(NC)]

    def credit(self, eng, who):
        eng.sem_inc(self.copied[who], self.who.count(who))

    def count(self, unit, c):
        who = self.who[c]
        return unit * self.who.count(who) + (self.who[:c + 1].count(who) + self.who.count(who))

    def wait_free(self, pe, unit, c):
        if c >= self.nbanks:
            pe.wait_ge(self.copied[self.who[c - self.nbanks]], self.count(unit, c - self.nbanks))
        else:
            before = max(k for k in range(NC) if k % self.nbanks == c)
            who = self.who[before]
            pe.wait_ge(self.copied[who], self.count(unit, before) - self.who.count(who))

    def wait_copied(self, pe, unit, c):
        pe.wait_ge(self.copied[self.who[c]], self.count(unit, c))

    def copy(self, eng, who, unit, c, bank, out):
        a, z = CHUNKS[c]
        eng.wait_ge(self.ready, unit * NC + (c + 1 + 2 * NC))
        if who == "act":
            ins = eng.activation(out[:, 0:z - a], bank[:, 0:z - a], ACT.Copy)
        else:
            ins = eng.tensor_copy(out[:, 0:z - a], bank[:, 0:z - a])
        ins.then_inc(self.copied[who], 1)


def graph_attention(nc, G):
    HEADS, CH, SLOPE, EPS = 4, 32, 0.2, 1e-5
    HW = CH + 1
    VW = 64
    BY_RELU = (1, 3)
    HALVES = ((0, 4), (4, NC))
    FINITE = 3.0e38
    with ExitStack() as ctx:
        sem = lambda name: ctx.enter_context(nc.semaphore(name))
        sbo = lambda name, shape, dt=FP32: ctx.enter_context(nc.sbuf_tensor(name, shape, dt))
        x, h, ident = G["x"], G["h"], G["ident"]
        res = sbo("res", [T, NT, D])
        vals = G["h_mem"][:, 0:NT * D].rearrange("p (t h w) -> p t h w", t=NT, h=HEADS)
        a_own = sbo("a_own", [T, NT, 2 * HEADS])
        a_long = sbo("a_long", [T, NT, HEADS])
        a_short = sbo("a_short", [T, NT, HEADS])
        greatest = sbo("greatest", [T, NT, HEADS])
        e_own = sbo("e_own", [T, NT, HEADS])
        sums = G["agg"][0:T, :].rearrange("p (t h w) -> p t h w", t=NT, h=HEADS)
        with ExitStack() as rows_stack:
            sbr = lambda name, shape, dt=FP32: rows_stack.enter_context(nc.sbuf_tensor(name, shape, dt))
            a_row = sbr("a_row", [T, HEADS, N])
            with ExitStack() as pre:
                sb = lambda name, shape, dt=FP32: pre.enter_context(nc.sbuf_tensor(name, shape, dt))
                cols = sb("cols2", [128, N])
                vcols = sb("vcols2", [128, N])
                w = sb("w2", [D, D])
                wres = sb("wres", [D, D])
                att = sb("att", [D, 2 * HEADS])
                att_wide = sb("att_wide", [D, HEADS, T])
                banks = bank_set(nc, pre, "l2pre", [
                    ("h", NC, "act"), ("vcols", NC, "act"), ("vals", NC, "dve"), ("res", NC, "dve")] +
                    [(f"row{k}", NC, "act") for k in range(HEADS)] + [("own", 1, "dve")])
                weights_in = sem("l2_weights_in")
                att_zero = sem("att_zero")
                att_made = sem("att_made")
                pre_dve = sem("l2pre_dve")
                with nc.Block() as block:
                    @block.sync
                    def _(sp):
                        sp.dma_start(w[:, :], G["L2_gnn_W"]).then_inc(weights_in, 16)
                        sp.dma_start(wres[:, :], G["L2_gnn_W_res"]).then_inc(weights_in, 16)
                        sp.wait_ge(att_zero, 1)
                        for k, name in enumerate(("L2_gnn_att_src", "L2_gnn_att_dst")):
                            for j in range(HEADS):
                                with nc.allow_non_contiguous_dma(reason="small weights"):
                                    sp.dma_start(att[j * CH:(j + 1) * CH, k * HEADS + j:k * HEADS + j + 1],
                                                 G[name][j:j + 1, :].rearrange("a c -> c a")).then_inc(weights_in, 16)

                    @block.gpsimd
                    def _(pool):
                        pool.memset(att[:, :], 0.0).then_inc(att_zero, 1)

                    @block.tensor
                    def _(pe):
                        pe_turn(pe, banks, "h", h, D, ident)
                        banks.done(pe, "h")
                        pe.wait_ge(weights_in, 160)
                        pe_columns(pe, banks, "vcols", w[:, :], cols)
                        pe_rows(pe, banks, "vals", [cols], [w[:, :]])
                        pe_rows(pe, banks, "res", [cols], [wres[:, :]])
                        banks.done(pe, "vcols")
                        pe.wait_ge(att_made, 1)
                        for k in range(HEADS):
                            pe_columns(pe, banks, f"row{k}", att_wide[:, k, :], vcols)
                        bank = banks.fill(pe, "own", 0)
                        for t in range(NT):
                            last = pe.matmul(bank[0:T, 8 * t:8 * t + 8], vcols[:, t * T:(t + 1) * T], att[:, :], start=True, stop=True)
                        last.then_inc(banks.filled, 1)

                    @block.scalar
                    def _(act):
                        act_columns(act, banks, "h", cols)
                        act_columns(act, banks, "vcols", vcols)
                        for k in range(HEADS):
                            act_columns(act, banks, f"row{k}", a_row[:, k, :], rows=T)

                    @block.vector
                    def _(dve):
                        m = Marks(pre_dve)
                        dve.wait_ge(weights_in, 160)
                        dve.tensor_copy(att_wide[:, :, :], att[:, 0:HEADS].unsqueeze(2).broadcast_to([D, HEADS, T])).then_inc(att_made, 1)
                        for name, out in (("vals", vals.rearrange("p t h w -> p t (h w)")), ("res", res)):
                            for c in range(NC):
                                ts = tiles_of(c)
                                bank = banks.full(dve, name, c)
                                dve.tensor_copy(out[:, ts[0]:ts[-1] + 1, :], rows_view(bank, c, D)).then_inc(banks.read["dve"], 1)
                        bank = banks.full(dve, "own", 0)
                        dve.tensor_copy(a_own[:, :, :], bank[0:T, 0:NT * 8].rearrange("p (t k) -> p t k", k=8)).then_inc(banks.read["dve"], 1)
                        banks.done(dve, "own", 1)
                        chain(dve, m, dve.tensor_scalar(a_long[:, :, :], a_own[:, :, 0:HEADS], 1.0 - SLOPE, None, ALU.mult))
                        chain(dve, m, dve.tensor_scalar(a_short[:, :, :], a_own[:, :, 0:HEADS], SLOPE, None, ALU.mult))

            with ExitStack() as maxima:
                sb = lambda name, shape, dt=FP32: maxima.enter_context(nc.sbuf_tensor(name, shape, dt))
                bias = [sb(f"bias{p}", [T, N]) for p in range(2)]
                masked = [sb(f"masked{k}", [T, N]) for k in range(2)]
                top = [sb(f"top{p}", [T, HEADS]) for p in range(2)]
                bias_in = [sem(f"bias_in{p}") for p in range(2)]
                top_done = sem("top_done")
                top_kept = sem("top_kept")
                with nc.Block() as block:
                    @block.sync
                    def _(sp):
                        sp.dma_start(bias[0][:, :], G["bias_dram"][0, :, :]).then_inc(bias_in[0], 16)
                        sp.dma_start(bias[1][:, :], G["bias_dram"][1, :, :]).then_inc(bias_in[1], 16)

                        def load(b, p):
                            sp.wait_ge(top_done, HEADS * b - HEADS + 1)
                            sp.dma_start(bias[p][:, :], G["bias_dram"][b, :, :]).then_inc(bias_in[p], 16)
                        with sp.Fori(1, NT // 2) as i:
                            load(2 * i, 0)
                            load(2 * i + 1, 1)
                        load(NT - 1, 0)

                    @block.scalar
                    def _(act):
                        def step(b, p, i2):
                            act.wait_ge(top_done, HEADS * b + HEADS + 1)
                            act.activation(greatest[:, bass.ds(b, 1), :], top[p][:, :].unsqueeze(1), ACT.Copy).then_inc(top_kept, 1)
                        act.sem_inc(top_kept, 2)
                        pairs_of_blocks(act, step)

                    @block.vector
                    def _(dve):
                        def step(b, p, i2):
                            dve.wait_ge(bias_in[p], 16 * i2 + 16)
                            dve.wait_ge(top_kept, b + 1)
                            for k in range(HEADS):
                                dve.wait_ge(top_done, HEADS * b + (k + 1))
                                dve.sem_inc(G["passed"], 1)
                                dve.tensor_tensor_reduce(out=masked[k % 2][:, :], in0=a_row[:, k, :], in1=bias[p][:, :], scale=1.0,
                                                         scalar=-3.0e38, op0=ALU.add, op1=ALU.max,
                                                         accum_out=top[p][:, k:k + 1]).then_inc(top_done, 1)
                        dve.sem_inc(top_done, 1)
                        pairs_of_blocks(dve, step)

        with ExitStack() as loop:
            sb = lambda name, shape, dt=FP32: loop.enter_context(nc.sbuf_tensor(name, shape, dt))
            p_row = sb("p_row", [T, HEADS, N])
            q_row = sb("q_row", [T, HEADS, N])
            rows_in = [[sem(f"rows_in{half}_{k}") for k in range(HEADS)] for half in range(2)]
            with ExitStack() as prep:
                sbp = lambda name, shape, dt=FP32: prep.enter_context(nc.sbuf_tensor(name, shape, dt))
                pq = sbp("pq", [T, 2, HEADS, NT])
                pq_turned = sbp("pq_turned", [HEADS * NT, 2, T])
                pq_ps = prep.enter_context(nc.psum_tensor("pq_ps", [HEADS * NT, 2, T], FP32))
                logit = sbp("logit", [T, NT, HEADS])
                pq_made, pq_ready, pq_copied, pq_out = sem("pq_made"), sem("pq_ready"), sem("pq_copied"), sem("pq_out")
                own_made = sem("own_made")
                prep_dve = sem("l2prep_dve")
                with nc.Block() as block:
                    @block.vector
                    def _(dve):
                        m = Marks(prep_dve)
                        src, dst = a_own[:, :, 0:HEADS], a_own[:, :, HEADS:]
                        pq_of = lambda k: pq[:, k, :, :].rearrange("p h t -> p t h")
                        lrelu = lambda v: chain(dve, m, dve.scalar_tensor_tensor(out=v, in0=v, scalar=SLOPE, in1=v,
                                                                                 op0=ALU.mult, op1=ALU.max))
                        chain(dve, m, dve.tensor_tensor(greatest[:, :, :], greatest[:, :, :], src, ALU.max))
                        chain(dve, m, dve.tensor_tensor(greatest[:, :, :], greatest[:, :, :], dst, ALU.add))
                        lrelu(greatest[:, :, :])
                        chain(dve, m, dve.tensor_tensor(pq_of(0), dst, greatest[:, :, :], ALU.subtract))
                        chain(dve, m, dve.scalar_tensor_tensor(out=pq_of(1), in0=dst, scalar=SLOPE, in1=greatest[:, :, :],
                                                               op0=ALU.mult, op1=ALU.subtract))
                        for k in BY_RELU:
                            chain(dve, m, dve.tensor_scalar(pq[:, 0, k, :], a_own[:, :, HEADS + k], 1.0 - SLOPE, None, ALU.mult))
                        dve.sem_inc(pq_made, 1)
                        chain(dve, m, dve.tensor_tensor(logit[:, :, :], src, dst, ALU.add))
                        lrelu(logit[:, :, :])
                        dve.tensor_tensor(logit[:, :, :], logit[:, :, :], greatest[:, :, :], ALU.subtract).then_inc(own_made, 1)

                    @block.tensor
                    def _(pe):
                        pe.wait_ge(pq_made, 1)
                        for k in range(2):
                            pe.transpose(pq_ps[:, k, :], pq[:, k, :, :].rearrange("p h t -> p (h t)"), ident[0:T, 0:T]
                                         ).then_inc(pq_ready, 1)

                    @block.scalar
                    def _(act):
                        act.wait_ge(pq_ready, 2)
                        act.activation(pq_turned[:, :, :], pq_ps[:, :, :], ACT.Copy).then_inc(pq_copied, 1)
                        act.wait_ge(own_made, 1)
                        act.activation(e_own[:, :, :], logit[:, :, :], ACT.Exp)

                    @block.sync
                    def _(sp):
                        sp.wait_ge(pq_copied, 1)
                        sp.dma_start(G["pq_dram"].rearrange("k a p -> a k p"), pq_turned[:, :, :]).then_inc(pq_out, 16)
                        sp.wait_ge(pq_out, 16)
                        for half, (c0, c1) in enumerate(HALVES):
                            a, z = CHUNKS[c0][0], CHUNKS[c1 - 1][1]
                            for k in range(HEADS):
                                for j, row in enumerate((p_row, q_row)):
                                    line = G["pq_dram"][j, :, :].rearrange("(h t) p -> h (t p)", h=HEADS)[k:k + 1, a:z]
                                    sp.dma_start(row[:, k, a:z], line.broadcast_to([T, z - a])).then_inc(rows_in[half][k], 16)

            CW = CHUNKS[HALVES[0][1]][0]
            z_buf = [sb(f"weights{k}", [128, CW]) for k in range(HEADS)]
            counts = [sb(f"l2counts{p}", [T, CW]) for p in range(2)]
            v_tile = [sb(f"v_tile{p}", [T, HEADS, VW]) for p in range(2)]
            acc = [[loop.enter_context(nc.psum_tensor(f"gat_sum{j}_{c}", [128, 512], FP32)) for c in range(4)] for j in range(2)]
            counts_in = [sem(f"l2counts_in{p}") for p in range(2)]
            ones_set = sem("ones_set")
            v_staged = sem("v_staged")
            max_made = sem("max_made")
            relu_made = sem("relu_made")
            relu_added = sem("relu_added")
            exp_made = sem("exp_made")
            w_made = sem("w_made")
            w_used = sem("w_used")
            out_copied = sem("gat_out_copied")
            out_turned = sem("gat_out_turned")
            at = lambda v, t, k: v[:, bass.ds(t, 1), k:k + 1].rearrange("p a k -> p (a k)")
            for half, (c0, c1) in enumerate(HALVES):
                a0, z0 = CHUNKS[c0][0], CHUNKS[c1 - 1][1]
                width = z0 - a0
                T0 = half * NT
                U0 = HEADS * T0
                with nc.Block() as block:
                    @block.sync
                    def _(sp):
                        def load(t, p):
                            sp.dma_start(counts[p][:, 0:width], G["counts_dram"][t, :, a0:z0]).then_inc(counts_in[p], 16)
                        load(0, 0)
                        load(1, 1)

                        def next_load(t, p):
                            sp.wait_ge(w_made, U0 + HEADS * t - HEADS)
                            load(t, p)
                        with sp.Fori(1, NT // 2) as i:
                            next_load(2 * i, 0)
                            next_load(2 * i + 1, 1)
                        next_load(NT - 1, 0)

                    @block.gpsimd
                    def _(pool):
                        if half == 0:
                            for p in range(2):
                                pool.memset(v_tile[p][:, :, CH:], 1.0).then_inc(ones_set, 1)
                        for k in BY_RELU:
                            pool.wait_ge(rows_in[half][k], 32)

                        def add(t, n):
                            pool.wait_ge(relu_made, 2 * (T0 + t) + (n + 1))
                            z = z_buf[BY_RELU[n]][0:T, 0:width]
                            pool.tensor_tensor(z, z, q_row[:, BY_RELU[n], a0:z0], ALU.add).then_inc(relu_added, 1)

                        def step(t, p, guard=True):
                            add(t, 0)
                            if guard:
                                pool.wait_ge(w_used, U0 + HEADS * t - HEADS)
                                pool.sem_inc(G["passed"], 1)
                            pool.tensor_copy(v_tile[p][:, :, 0:CH].unsqueeze(1), vals[:, bass.ds(t, 1), :, :]).then_inc(v_staged, 1)
                            add(t, 1)
                        step(0, 0, guard=False)
                        step(1, 1, guard=False)
                        with pool.Fori(1, NT // 2) as i:
                            step(2 * i, 0)
                            step(2 * i + 1, 1)
                        step(NT - 1, 0)

                    @block.scalar
                    def _(act):
                        def exponential(t, k):
                            if k in BY_RELU:
                                act.wait_ge(relu_added, 2 * (T0 + t) + (BY_RELU.index(k) + 1))
                            else:
                                act.wait_ge(max_made, 2 * (T0 + t) + (k // 2 + 1))
                            z = z_buf[k][0:T, 0:width]
                            act.activation(z, z, ACT.Exp, bias=at(a_short, t, k)).then_inc(exp_made, 1)

                        def relu(t, k, first=False):
                            if not first:
                                act.wait_ge(w_used, U0 + HEADS * t + (k + 1 - HEADS))
                            act.activation(z_buf[k][0:T, 0:width], p_row[:, k, a0:z0], ACT.Relu,
                                           bias=at(a_long, t, k)).then_inc(relu_made, 1)

                        def step(t, first=False, last=False):
                            exponential(t, 0)
                            relu(t, 3, first)
                            for k in range(1, HEADS):
                                exponential(t, k)
                            if not last:
                                relu(t + 1, 1)
                        act.preload_act_table(ACT.Exp)
                        for k in BY_RELU:
                            act.wait_ge(rows_in[half][k], 32)
                        relu(0, 1, first=True)
                        step(0, first=True)
                        with act.Fori(1, NT - 1) as t:
                            step(t)
                        step(NT - 1, last=True)

                    @block.vector
                    def _(dve):
                        def maximum(t, k, first=False):
                            if not first:
                                dve.wait_ge(w_used, U0 + HEADS * t + (k + 1 - HEADS))
                            dve.scalar_tensor_tensor(out=z_buf[k][0:T, 0:width], in0=p_row[:, k, a0:z0], scalar=at(a_long, t, k),
                                                     in1=q_row[:, k, a0:z0], op0=ALU.add, op1=ALU.max).then_inc(max_made, 1)

                        def weight(t, p, i2, k):
                            if k == 0:
                                dve.wait_ge(counts_in[p], 16 * i2 + 16 * ((NT + 1 - p) // 2 * half + 1))
                            dve.wait_ge(exp_made, U0 + HEADS * t + (k + 1))
                            z = z_buf[k][0:T, 0:width]
                            dve.scalar_tensor_tensor(out=z, in0=z, scalar=FINITE, in1=counts[p][:, 0:width],
                                                     op0=ALU.min, op1=ALU.mult).then_inc(w_made, 1)

                        def step(t, p, i2, first=False, last=False):
                            weight(t, p, i2, 0)
                            if first:
                                dve.wait_ge(rows_in[half][2], 32)
                            maximum(t, 2, first)
                            weight(t, p, i2, 1)
                            weight(t, p, i2, 2)
                            if not last:
                                maximum(t + 1, 0)
                            weight(t, p, i2, 3)
                        dve.wait_ge(rows_in[half][0], 32)
                        maximum(0, 0, first=True)
                        step(0, 0, 0, first=True)
                        with dve.Fori(0, NT // 2 - 1) as i:
                            step(2 * i + 1, 1, i)
                            step(2 * i + 2, 0, i + 1)
                        step(NT - 2, 1, NT // 2 - 1)
                        step(NT - 1, 0, NT // 2, last=True)

                    @block.tensor
                    def _(pe):
                        if half == 0:
                            pe.wait_ge(ones_set, 2)

                        def tile(t, p, first=False, last=False):
                            pe.wait_ge(v_staged, T0 + t + 1)
                            for k in range(HEADS):
                                pe.wait_ge(w_made, U0 + HEADS * t + (k + 1))
                                rows = slice(VW * (k % 2), VW * (k % 2) + VW)
                                for c in range(c0, c1):
                                    a, z = CHUNKS[c]
                                    done = pe.matmul(acc[k // 2][c - c0][rows, 0:z - a], v_tile[p][:, k, :], z_buf[k][0:T, a - a0:z - a0],
                                                     start=first, stop=last)
                                done.then_inc(w_used, 1)
                        tile(0, 0, first=True)
                        with pe.Fori(0, NT // 2 - 1) as i:
                            tile(2 * i + 1, 1)
                            tile(2 * i + 2, 0)
                        tile(NT - 2, 1)
                        tile(NT - 1, 0, last=True)

                with nc.Block() as block:
                    BANKS0 = 2 * HALVES[0][1] * half
                    @block.scalar
                    def _(act):
                        for j in range(2):
                            for c in range(c0, c1):
                                a, z = CHUNKS[c]
                                act.activation(z_buf[j][:, a - a0:z - a0], acc[j][c - c0][:, 0:z - a], ACT.Copy).then_inc(out_copied, 1)

                    @block.tensor
                    def _(pe):
                        for j in range(2):
                            for c in range(c0, c1):
                                pe.wait_ge(out_copied, BANKS0 + j * (c1 - c0) + c - c0 + 1)
                                for i in range(len(tiles_of(c))):
                                    at_col = CHUNKS[c][0] - a0 + i * T
                                    last = pe.transpose(acc[j][c - c0][0:T, i * 128:(i + 1) * 128], z_buf[j][:, at_col:at_col + T], ident[:, :])
                                last.then_inc(out_turned, 1)

                    @block.vector
                    def _(dve):
                        for j in range(2):
                            for c in range(c0, c1):
                                ts = tiles_of(c)
                                dve.wait_ge(out_turned, BANKS0 + j * (c1 - c0) + c - c0 + 1)
                                dve.tensor_copy(sums[:, ts[0]:ts[-1] + 1, 2 * j:2 * j + 2, :],
                                                acc[j][c - c0][0:T, 0:len(ts) * 128].rearrange("p (t h w) -> p t h w", h=2, w=VW)[:, :, :, 0:HW])

        with ExitStack() as post:
            sb = lambda name, shape, dt=FP32: post.enter_context(nc.sbuf_tensor(name, shape, dt))
            work = sb("work2", [T, NT, D])
            stat = sb("stat2", [T, 4, NT])
            total = sb("total", [T, NT, HEADS])
            rows = sb("rows2", [T, 5, D])
            rows_in = sem("l2_rows_in")
            root_in, root_out = sem("l2_root_in"), sem("l2_root_out")
            elu_in, elu_out = sem("elu_in"), sem("elu_out")
            post_dve = sem("l2post_dve")
            norm = Norm(sem, "norm3", stat, x, h, work)
            with nc.Block() as block:
                @block.sync
                def _(sp):
                    for k, name in enumerate(("bias", "bn_gamma", "bn_beta", "bn_mean", "bn_var")):
                        sp.dma_start(rows[:, k, :], G[f"L2_gnn_{name}"].unsqueeze(0).broadcast_to([T, D])).then_inc(rows_in, 16)

                @block.scalar
                def _(act):
                    act.wait_ge(root_in, 1)
                    act.activation(rows[:, 4, :], rows[:, 4, :], ACT.Sqrt).then_inc(root_out, 1)
                    act.wait_ge(elu_in, 1)
                    act.activation(work[:, :, :], work[:, :, :], ACT.Exp).then_inc(elu_out, 1)
                    norm.scalar(act)

                @block.vector
                def _(dve):
                    m = Marks(post_dve)
                    every = lambda k: rows[:, k, :].unsqueeze(1).broadcast_to([T, NT, D])
                    w4 = work[:, :, :].rearrange("p t (h w) -> p t h w", h=HEADS)
                    dve.wait_ge(rows_in, 80)
                    dve.tensor_scalar(rows[:, 4, :], rows[:, 4, :], EPS, None, ALU.add).then_inc(root_in, 1)
                    chain(dve, m, dve.tensor_tensor(total[:, :, :], sums[:, :, :, CH], e_own[:, :, :], ALU.add))
                    chain(dve, m, dve.reciprocal(total[:, :, :], total[:, :, :]))
                    for k in range(HEADS):
                        chain(dve, m, dve.tensor_tensor(w4[:, :, k, :], vals[:, :, k, :],
                                                        e_own[:, :, k].unsqueeze(2).broadcast_to([T, NT, CH]), ALU.mult))
                        chain(dve, m, dve.tensor_tensor(w4[:, :, k, :], w4[:, :, k, :], sums[:, :, k, 0:CH], ALU.add))
                        chain(dve, m, dve.tensor_tensor(w4[:, :, k, :], w4[:, :, k, :],
                                                        total[:, :, k].unsqueeze(2).broadcast_to([T, NT, CH]), ALU.mult))
                    chain(dve, m, dve.tensor_tensor(work[:, :, :], work[:, :, :], res[:, :, :], ALU.add))
                    bias, gamma, beta, mean, root = (rows[:, k, :] for k in range(5))
                    dve.wait_ge(root_out, 1)
                    chain(dve, m, dve.tensor_tensor(bias, bias, mean, ALU.subtract))
                    chain(dve, m, dve.reciprocal(root, root))
                    chain(dve, m, dve.tensor_tensor(gamma, gamma, root, ALU.mult))
                    chain(dve, m, dve.tensor_tensor(bias, bias, gamma, ALU.mult))
                    chain(dve, m, dve.tensor_tensor(beta, beta, bias, ALU.add))
                    chain(dve, m, dve.tensor_tensor(work[:, :, :], work[:, :, :], every(1), ALU.mult))
                    chain(dve, m, dve.tensor_tensor(work[:, :, :], work[:, :, :], every(2), ALU.add))
                    chain(dve, m, dve.tensor_scalar(res[:, :, :], work[:, :, :], 0.0, -1.0, ALU.max, ALU.add))
                    dve.tensor_scalar(work[:, :, :], work[:, :, :], 0.0, None, ALU.min).then_inc(elu_in, 1)
                    chain(dve, m, dve.tensor_tensor(x[:, :, :], x[:, :, :], res[:, :, :], ALU.add))
                    dve.wait_ge(elu_out, 1)
                    chain(dve, m, dve.tensor_tensor(x[:, :, :], x[:, :, :], work[:, :, :], ALU.add))
                    norm.vector(dve, m)


def transformer(nc, G):
    LAYERS, EPS = 4, 1e-5
    SCALE = float(1.0 / np.sqrt(D))
    S_BANKS = T_BANKS = 3
    with ExitStack() as ctx:
        sbo = lambda name, shape, dt=FP32: ctx.enter_context(nc.sbuf_tensor(name, shape, dt))
        x, h, ident, msg_mem = G["x"], G["h"], G["ident"], G["agg"]
        msg = msg_mem[0:T, 0:NT * D].rearrange("p (t d) -> p t d", d=D)
        cols = sbo("cols3", [128, N])
        work = sbo("work3", [T, NT, D])
        stat = sbo("stat3", [T, 4, NT])

        def every(v):
            return v.unsqueeze(1).broadcast_to([T, NT, D])

        def project(tag, w_src, b_src, into_x):
            with ExitStack() as pre:
                w = pre.enter_context(nc.sbuf_tensor(f"w_{tag}", [D, D], FP32))
                b = pre.enter_context(nc.sbuf_tensor(f"b_{tag}", [T, D], FP32))
                banks = bank_set(nc, pre, tag, [("h", NC, "act"), ("out", NC, "dve")])
                loaded = pre.enter_context(nc.semaphore(f"{tag}_loaded"))
                added = pre.enter_context(nc.semaphore(f"{tag}_added"))
                stored = pre.enter_context(nc.semaphore(f"{tag}_stored"))
                with nc.Block() as block:
                    @block.sync
                    def _(sp):
                        sp.dma_start(w[:, :], w_src).then_inc(loaded, 16)
                        sp.dma_start(b[:, :], b_src.unsqueeze(0).broadcast_to([T, D])).then_inc(loaded, 16)
                        if into_x:
                            sp.wait_ge(added, NC)
                            sp.dma_start(G["out"].rearrange("(t p) d -> p t d", p=T), x[:, :, :]).then_inc(stored, 16)
                            sp.wait_ge(stored, 16)

                    @block.tensor
                    def _(pe):
                        pe_turn(pe, banks, "h", h, D, ident)
                        banks.done(pe, "h")
                        pe.wait_ge(loaded, 32)
                        pe_rows(pe, banks, "out", [cols], [w[:, :]])

                    @block.scalar
                    def _(act):
                        act_columns(act, banks, "h", cols)

                    @block.vector
                    def _(dve):
                        dve.wait_ge(loaded, 32)
                        for c in range(NC):
                            ts = tiles_of(c)
                            bank = banks.full(dve, "out", c)
                            wide = b[:, :].unsqueeze(1).broadcast_to([T, len(ts), D])
                            part = slice(ts[0], ts[-1] + 1)
                            if into_x:
                                dve.tensor_tensor(work[:, part, :], rows_view(bank, c, D), wide, ALU.add).then_inc(banks.read["dve"], 1)
                                dve.wait_ge(banks.read["dve"], c + 1)
                                dve.tensor_tensor(x[:, part, :], x[:, part, :], work[:, part, :], ALU.add).then_inc(added, 1)
                            else:
                                dve.tensor_tensor(h[:, part, :], rows_view(bank, c, D), wide, ALU.add).then_inc(banks.read["dve"], 1)

        project("node_in", G["L3_gnn_Wn"], G["L3_gnn_bn"], False)

        with ExitStack() as lctx:
            sb = lambda name, shape, dt=FP32: lctx.enter_context(nc.sbuf_tensor(name, shape, dt))
            w = sb("w3", [D, 4, D])
            bq = sb("bq", [D, 2])
            rows = sb("rows3", [T, 4, D])
            q = sb("q", [D, N])
            k_high = sb("k_high", [D, N + 1], FP32R)
            k_low = sb("k_low", [D, N + 1], FP32R)
            vals = sb("vals3", [T, NT, D + 1])
            with nc.Fori(0, LAYERS) as l:
                used = []

                with ExitStack() as pre:
                    banks = bank_set(nc, pre, "qkv", [
                        ("h", NC, "act"), ("q", NC, "act"), ("k", NC, "dve"), ("v", NC, "dve")])
                    loaded = pre.enter_context(nc.semaphore("qkv_loaded"))
                    scaled = pre.enter_context(nc.semaphore("bq_scaled"))
                    high_made = pre.enter_context(nc.semaphore("k_high_made"))
                    k_all = pre.enter_context(nc.sbuf_tensor("k_all", [D, N], FP32))
                    used += [banks.filled, *banks.read.values(), loaded, scaled, high_made]
                    with nc.Block() as block:
                        @block.sync
                        def _(sp):
                            for j, name in enumerate(("WQ", "WK", "WV", "WO")):
                                sp.dma_start(w[:, j, :], G[f"L3_gnn_{name}"][l, :, :]).then_inc(loaded, 16)
                            for j, name in enumerate(("bQ", "bK")):
                                with nc.allow_non_contiguous_dma(reason="a bias as a column"):
                                    sp.dma_start(bq[:, j:j + 1], G[f"L3_gnn_{name}"][bass.ds(l, 1), :].rearrange("a d -> d a")).then_inc(loaded, 16)
                            for j, name in enumerate(("bV", "bO", "ln_g", "ln_b")):
                                sp.dma_start(rows[:, j, :], G[f"L3_gnn_{name}"][bass.ds(l, 1), :].broadcast_to([T, D])).then_inc(loaded, 16)

                        @block.gpsimd
                        def _(pool):
                            pool.memset(vals[:, :, D:D + 1], 1.0)
                            for part in (k_high, k_low):
                                pool.memset(part[:, N:N + 1].bitcast(FP32), 0.0)

                        @block.tensor
                        def _(pe):
                            pe_turn(pe, banks, "h", h, D, ident)
                            banks.done(pe, "h")
                            pe.wait_ge(loaded, 160)
                            pe_columns(pe, banks, "q", w[:, 0, :], cols)
                            pe_columns(pe, banks, "k", w[:, 1, :], cols)
                            pe_rows(pe, banks, "v", [cols], [w[:, 2, :]])

                        @block.scalar
                        def _(act):
                            act_columns(act, banks, "h", cols)
                            act.wait_ge(scaled, 1)
                            act_columns(act, banks, "q", q, bias=bq[:, 0:1], scale=SCALE)
                            for c, (a, z) in enumerate(CHUNKS):
                                banks.done(act, "k", c + 1)
                                act.activation(k_high[:, a:z], k_all[:, a:z], ACT.Copy).then_inc(high_made, 1)

                        @block.vector
                        def _(dve):
                            dve.wait_ge(loaded, 160)
                            dve.tensor_scalar(bq[:, 0:1], bq[:, 0:1], SCALE, None, ALU.mult).then_inc(scaled, 1)
                            for c, (a, z) in enumerate(CHUNKS):
                                bank = banks.full(dve, "k", c)
                                dve.tensor_scalar(k_all[:, a:z], bank[:, 0:z - a], bq[:, 1:2], None, ALU.add).then_inc(banks.read["dve"], 1)
                            for c, (a, z) in enumerate(CHUNKS):
                                dve.wait_ge(high_made, c + 1)
                                dve.tensor_tensor(k_low[:, a:z], k_all[:, a:z], k_high[:, a:z].bitcast(FP32), ALU.subtract)
                            for c in range(NC):
                                ts = tiles_of(c)
                                bank = banks.full(dve, "v", c)
                                dve.tensor_tensor(vals[:, ts[0]:ts[-1] + 1, 0:D], rows_view(bank, c, D),
                                                  rows[:, 0, :].unsqueeze(1).broadcast_to([T, len(ts), D]), ALU.add
                                                  ).then_inc(banks.read["dve"], 1)

                with ExitStack() as loop:
                    lsb = lambda name, shape, dt=FP32: loop.enter_context(nc.sbuf_tensor(name, shape, dt))
                    ps = lambda name, shape, dt=FP32: loop.enter_context(nc.psum_tensor(name, shape, dt))

                    def sem(name):
                        s = loop.enter_context(nc.semaphore(name))
                        used.append(s)
                        return s
                    row = [lsb(f"arow{p}", [T, N]) for p in range(2)]
                    bias = [lsb(f"abias{p}", [T, N]) for p in range(2)]
                    wcol = [lsb(f"awcol{k}", [T, C4]) for k in range(T_BANKS)]
                    q_high = [lsb(f"q_high{p}", [D, T], FP32R) for p in range(2)]
                    q_low = [lsb(f"q_low{p}", [D, T], FP32R) for p in range(2)]
                    top = [lsb(f"atop{p}", [T, NC]) for p in range(2)]
                    neg = [lsb(f"aneg{p}", [T, 1]) for p in range(2)]
                    inv = [lsb(f"ainv{p}", [T, 1]) for p in range(2)]
                    s_ps = [ps(f"scores{k}", [T, C4]) for k in range(S_BANKS)]
                    bank = [ps(f"aturned{k}", [T, C4]) for k in range(T_BANKS)]
                    sum_ps = [ps(f"asum{p}", [T, D + 1]) for p in range(2)]
                    bias_in = [sem(f"abias_in{p}") for p in range(2)]
                    q_staged = sem("q_staged")
                    scores_ready = sem("scores_ready")
                    scores_read = sem("scores_read")
                    max_done = sem("amax_done")
                    exp_done = sem("aexp_done")
                    sum_ready = sem("asum_ready")
                    sum_read = sem("asum_read")
                    inv_done = sem("ainv_done")
                    turned = Turned(T_BANKS, sem("aturned_ready"), {k: sem(f"acopied_{k}") for k in ("act", "dve")},
                                    ACT_COPIES["attention"])

                    AHEAD = 2

                    def ahead(b, p, c, act_on):
                        to, q, c = (b + 1, 1 - p, c + AHEAD) if c + AHEAD < NC else (b + 2, p, c + AHEAD - NC)
                        if not (isinstance(to, int) and to >= NT):
                            act_on(to, q, c)

                    def over_blocks(eng, step):
                        with eng.Fori(0, NT // 2 - 1) as i:
                            step(2 * i, 0)
                            step(2 * i + 1, 1)
                        for b in range(NT - 3, NT):
                            step(b, b % 2)

                    with nc.Block() as block:
                        @block.sync
                        def _(sp):
                            def step(b, p, i2):
                                sp.wait_ge(scores_read, b * NC + 1)
                                sp.dma_start(bias[p][:, :], G["bias_dram"][b, :, :]).then_inc(bias_in[p], 16)
                            pairs_of_blocks(sp, step)

                        @block.gpsimd
                        def _(pool):
                            def step(b, p, i2):
                                pool.wait_ge(scores_read, b * NC + 1)
                                pool.sem_inc(G["passed"], 1)
                                pool.tensor_copy(q_high[p][:, :], q[:, bass.ds(b * T, T)]).then_inc(q_staged, 1)
                                pool.wait_ge(q_staged, 2 * b + 1)
                                pool.sem_inc(G["passed"], 1)
                                pool.tensor_tensor(q_low[p][:, :], q[:, bass.ds(b * T, T)], q_high[p][:, :].bitcast(FP32),
                                                   ALU.subtract).then_inc(q_staged, 1)
                            pairs_of_blocks(pool, step)
                            pool.tensor_tensor(h[:, :, :], h[:, :, :], every(rows[:, 1, :]), ALU.add)

                        @block.tensor
                        def _(pe):
                            pe.sem_inc(turned.ready, 2 * NC)

                            def scores(b, p, c):
                                a, z = CHUNKS[c]
                                if c == 0:
                                    pe.wait_ge(q_staged, 2 * b + 2)
                                before = c - S_BANKS if c >= S_BANKS else max(k for k in range(NC) if k % S_BANKS == c) - NC
                                pe.wait_ge(scores_read, b * NC + (before + 1 + NC))
                                z += (z - a) % 2
                                terms = ((q_high, k_low), (q_low, k_high), (q_high, k_high))
                                for n, (left, right) in enumerate(terms):
                                    last = pe.matmul(s_ps[c % S_BANKS][:, 0:z - a], left[p][:, :], right[:, a:z],
                                                     start=(n == 0), stop=(n == len(terms) - 1))
                                last.then_inc(scores_ready, 1)

                            def weigh(b, p, c):
                                if c == 0:
                                    pe.wait_ge(sum_read, b + 1)
                                turned.wait_copied(pe, b, c)
                                for j, t in enumerate(tiles_of(c)):
                                    last = pe.matmul(sum_ps[p][:, :], wcol[c % T_BANKS][:, j * T:(j + 1) * T], vals[:, t, :],
                                                     start=(t == 0), stop=(t == NT - 1))
                                if c == NC - 1:
                                    last.then_inc(sum_ready, 1)

                            def turn(b, p, c):
                                pe.wait_ge(exp_done, b * NC + (c + 1))
                                turned.wait_free(pe, b, c)
                                for j, t in enumerate(tiles_of(c)):
                                    last = pe.transpose(bank[c % T_BANKS][:, j * T:(j + 1) * T], row[p][:, t * T:(t + 1) * T], ident[0:T, 0:T])
                                last.then_inc(turned.ready, 1)

                            def step(b, p):
                                for c in range(NC):
                                    ahead(b, p, c, scores)
                                    turn(b, p, c)
                                    if c:
                                        weigh(b, p, c - 1)
                                weigh(b, p, NC - 1)
                            for c in range(NC):
                                scores(0, 0, c)
                            for c in range(AHEAD):
                                scores(1, 1, c)
                            over_blocks(pe, step)

                        @block.scalar
                        def _(act):
                            turned.credit(act, "act")
                            act.preload_act_table(ACT.Exp)

                            def exponential(b, p, c):
                                if c == 0:
                                    act.wait_ge(max_done, b + 1)
                                a, z = CHUNKS[c]
                                act.activation(row[p][:, a:z], row[p][:, a:z], ACT.Exp, bias=neg[p][:, :]).then_inc(exp_done, 1)

                            def step(b, p):
                                for c in range(AHEAD, NC):
                                    exponential(b, p, c)
                                    if c in (2, 4):
                                        turned.copy(act, "act", b, c - 1, bank[(c - 1) % T_BANKS], wcol[(c - 1) % T_BANKS])
                                if not (isinstance(b, int) and b == NT - 1):
                                    for c in range(AHEAD):
                                        exponential(b + 1, 1 - p, c)
                                turned.copy(act, "act", b, 5, bank[5 % T_BANKS], wcol[5 % T_BANKS])
                            for c in range(AHEAD):
                                exponential(0, 0, c)
                            over_blocks(act, step)

                        @block.vector
                        def _(dve):
                            turned.credit(dve, "dve")
                            dve.sem_inc(scores_read, NC)
                            dve.sem_inc(sum_read, 2)

                            def maximum(b, p, c):
                                a, z = CHUNKS[c]
                                if c == 0:
                                    dve.wait_ge(bias_in[p], 8 * (b - p) + 16)
                                dve.wait_ge(turned.ready, b * NC + (c + 1))
                                dve.wait_ge(scores_ready, b * NC + (c + 1))
                                dve.sem_inc(G["passed"], 1)
                                dve.tensor_tensor_reduce(out=row[p][:, a:z], in0=s_ps[c % S_BANKS][:, 0:z - a], in1=bias[p][:, a:z],
                                                         scale=1.0, scalar=-3.0e38, op0=ALU.add, op1=ALU.max,
                                                         accum_out=top[p][:, c:c + 1]).then_inc(scores_read, 1)
                                if c == NC - 1:
                                    dve.wait_ge(scores_read, b * NC + 2 * NC)
                                    dve.sem_inc(G["passed"], 1)
                                    dve.tensor_reduce(neg[p][:, :], top[p][:, :], AX.X, ALU.max, negate=True).then_inc(max_done, 1)

                            def finish(b, p):
                                dve.wait_ge(sum_ready, b + 1)
                                dve.reciprocal(inv[p][:, :], sum_ps[p][:, D:D + 1]).then_inc(inv_done, 1)
                                dve.wait_ge(inv_done, b + 1)
                                dve.tensor_scalar(msg[:, bass.ds(b, 1), :], sum_ps[p][:, 0:D].unsqueeze(1), inv[p][:, :],
                                                  G["has_in"][:, bass.ds(b, 1)], ALU.mult, ALU.mult).then_inc(sum_read, 1)

                            def step(b, p):
                                for c in range(NC):
                                    ahead(b, p, c, maximum)
                                    if c not in ACT_COPIES["attention"]:
                                        turned.copy(dve, "dve", b, c, bank[c % T_BANKS], wcol[c % T_BANKS])
                                finish(b, p)
                            for c in range(NC):
                                maximum(0, 0, c)
                            for c in range(AHEAD):
                                maximum(1, 1, c)
                            over_blocks(dve, step)

                with ExitStack() as post:
                    banks = bank_set(nc, post, "attn_out", [("msg", NC, "act"), ("out", NC, "dve")])
                    psem = lambda name: post.enter_context(nc.semaphore(name))
                    post_done = psem("l3_post_dve")
                    normed = psem("l3_normed")
                    affine_done = psem("l3_affine_pool")
                    norm = Norm(psem, "l3_norm", stat, work, h, msg, relu=False)
                    used += [banks.filled, *banks.read.values(), post_done, normed, affine_done, *norm.sems]
                    SHARE = NT * 2 // 3
                    with nc.Block() as block:
                        @block.tensor
                        def _(pe):
                            pe_turn(pe, banks, "msg", msg, D, ident)
                            banks.done(pe, "msg")
                            pe_rows(pe, banks, "out", [cols], [w[:, 3, :]])

                        @block.scalar
                        def _(act):
                            act_columns(act, banks, "msg", cols)
                            norm.scalar(act)

                        def affine(eng, m, a, z):
                            for k, op in ((2, ALU.mult), (3, ALU.add)):
                                chain(eng, m, eng.tensor_tensor(h[:, a:z, :], h[:, a:z, :],
                                                                rows[:, k, :].unsqueeze(1).broadcast_to([T, z - a, D]), op))

                        @block.gpsimd
                        def _(pool):
                            pool.wait_ge(normed, 1)
                            affine(pool, Marks(affine_done), SHARE, NT)

                        @block.vector
                        def _(dve):
                            m = Marks(post_done)
                            for c in range(NC + 1):
                                if c < NC:
                                    ts = tiles_of(c)
                                    bank = banks.full(dve, "out", c)
                                    part = slice(ts[0], ts[-1] + 1)
                                    dve.tensor_tensor(work[:, part, :], rows_view(bank, c, D), h[:, part, :], ALU.add).then_inc(banks.read["dve"], 1)
                                if c:
                                    banks.done(dve, "out", c)
                                    for t in tiles_of(c - 1):
                                        last = norm.tile_statistics(dve, t)
                            chain(dve, m, last)
                            norm.vector(dve, m, have_statistics=True)
                            dve.sem_inc(normed, 1)
                            affine(dve, m, 0, SHARE)
                    with nc.Block() as block:
                        @block.sync
                        def _(sp):
                            for s in {s.num: s for s in used}.values():
                                sp.sem_clear(s)

        project("node_out", G["L3_gnn_Wout"], G["L3_gnn_bout"], True)


INPUTS = ["x", "src", "dst",
          "L0_gnn_W1", "L0_gnn_b1", "L0_gnn_W2", "L0_gnn_b2",
          "L1_gnn_W1", "L1_gnn_b1", "L1_gnn_W2", "L1_gnn_b2",
          "L2_gnn_W", "L2_gnn_att_src", "L2_gnn_att_dst", "L2_gnn_bias", "L2_gnn_W_res",
          "L2_gnn_bn_gamma", "L2_gnn_bn_beta", "L2_gnn_bn_mean", "L2_gnn_bn_var",
          "L3_gnn_Wn", "L3_gnn_bn", "L3_gnn_WQ", "L3_gnn_bQ", "L3_gnn_WK", "L3_gnn_bK",
          "L3_gnn_WV", "L3_gnn_bV", "L3_gnn_WO", "L3_gnn_bO", "L3_gnn_ln_g", "L3_gnn_ln_b",
          "L3_gnn_Wout", "L3_gnn_bout"]


def program(nc, ins, out):
    with ExitStack() as ctx:
        sb = lambda name, shape, dt=FP32: ctx.enter_context(nc.sbuf_tensor(name, shape, dt))
        dram = lambda name, shape, dt=FP32: nc.dram_tensor(name, shape, dt).ap()
        G = dict(ins)
        G["x_in"], G["out"] = ins["x"], out
        G["x"] = sb("x", [T, NT, D])
        G["h_mem"] = sb("h_mem", [T, NT * 132])
        G["h"] = G["h_mem"][:, 0:NT * D].rearrange("p (t d) -> p t d", d=D)
        G["agg"] = sb("agg", [128, NT * 132])
        G["deg"] = sb("deg", [T, NT])
        G["selfc"] = sb("selfc", [T, NT])
        G["ident"] = sb("ident", [128, 128])
        G["dinv"] = sb("dinv", [T, NT])
        G["has_in"] = sb("has_in", [T, NT])
        G["passed"] = ctx.enter_context(nc.semaphore("passed"))
        G["counts_dram"] = dram("counts_dram", [NT, T, N])
        G["bias_dram"] = dram("bias_dram", [NT, T, N])
        G["pq_dram"] = dram("pq_dram", [2, 4 * NT, T])
        with ExitStack() as edges:
            se = lambda name, shape, dt=FP32: edges.enter_context(nc.sbuf_tensor(name, shape, dt))
            G["key"] = se("key", [EP, PT * NPAIR])
            G["place"] = se("place", [EP, PT * NPAIR])
            G["gmin"] = se("gmin", [1, 2 * NPAIR])
            G["ranges"] = se("ranges", [1, 3 * NT], I32)
            G["iota_win"] = se("iota_win", [EP, WN], FP16)
            G["iota_t"] = se("iota_t", [EP, T], FP16)
            G["tiny"] = se("tiny", [128, 1])
            G["mm_dram"] = dram("mm_dram", [2, 2 * NPAIR])
            G["tab_dram"] = dram("tab_dram", [NT, 3], I32)
            prepare(nc, G)
            build_counts(nc, G)
        layers_0_1(nc, G)
        graph_attention(nc, G)
        transformer(nc, G)


def kernel(**inputs):
    from concourse import bacc
    from concourse.bass_utils import run_bass_kernel_spmd

    nc = bacc.Bacc("TRN2", target_bir_lowering=False, num_devices=1)
    arrays, ins = {}, {}
    for name in INPUTS:
        a = np.ascontiguousarray(inputs[name])
        arrays["in_" + name] = a
        ins[name] = nc.dram_tensor("in_" + name, a.shape, mybir.dt.from_np(a.dtype), kind="ExternalInput").ap()
    out = nc.dram_tensor("out", (N, D), FP32, kind="ExternalOutput").ap()
    program(nc, ins, out)
    return run_bass_kernel_spmd(nc, [arrays], core_ids=[0]).results[0]["out"]
```
